# Optimizing a Trainium2 kernel written in Bass

```python
import numpy as np
import jax
import jax.numpy as jnp

def _softmax(x, axis=-1):
    return jax.nn.softmax(x, axis=axis)

def _gelu(x):
    return jax.nn.gelu(x, approximate=True)

def _silu(x):
    return jax.nn.silu(x)

def _sigmoid(x):
    return jax.nn.sigmoid(x)

def _layernorm(x, axis=-1, eps=1e-05):
    m = jnp.mean(x, axis=axis, keepdims=True)
    v = jnp.var(x, axis=axis, keepdims=True)
    return (x - m) / jnp.sqrt(v + eps)

def _scatter_add(tgt, idx, src, axis=0):
    return tgt.at[idx].add(src)

def _segment_sum(src, seg, n):
    return jax.ops.segment_sum(src, seg, n)
kernel_name = 'mk_decoder_postln_d1_seqx_r8_92580d'

def setup_inputs(seed: int=0):
    np.random.seed(seed)
    _w = jnp.asarray

    def _rec_inputs():
        import jax
        import jax.numpy as jnp
        _rk = jax.random.key(seed)
        x = -0.0002928 + 1 * jax.random.normal(jax.random.fold_in(_rk, 1), (32, 56, 128), jnp.float32)
        _lenS = 56 - jax.random.randint(jax.random.fold_in(_rk, 7), (32,), 0, max(1, 56 // 4) + 1, jnp.int32)
        _lenS2 = 1500 - jax.random.randint(jax.random.fold_in(_rk, 8), (32,), 0, max(1, 1500 // 4) + 1, jnp.int32)
        _ctx_1024P = jax.random.normal(jax.random.fold_in(_rk, 11), (32, 16, 128), jnp.float32)
        _ctx_1024c = jax.random.dirichlet(jax.random.fold_in(_rk, 511), 0.3 * jnp.ones((16,), jnp.float32), (32, 1500))
        _ctx_1024t = jnp.einsum('bsk,bkd->bsd', _ctx_1024c, _ctx_1024P)
        _ctx_1024t = _ctx_1024t * jax.lax.rsqrt(jnp.mean(jnp.square(_ctx_1024t)) + 1e-12) * 0.953939
        ctx_1024 = -1.39393e-06 + 0.999914 * (_ctx_1024t + 0.3 * jax.random.normal(jax.random.fold_in(_rk, 611), (32, 1500, 128), jnp.float32))
        return (x, ctx_1024)
    x, ctx_1024 = _rec_inputs()

    def _L0_attn_setup():
        import jax, jax.numpy as jnp
        import numpy as np
        DIM = 128
        HEADS = 16
        HEAD_DIM = DIM // HEADS
        FEAT = 32
        B, N = (4, 512)

        def _elu1(x):
            return jnp.where(x > 0, x + 1.0, jnp.exp(x))
        key = jax.random.key(seed)
        k_x, k_qkv, k_proj, k_wo, k_bo = jax.random.split(key, 5)
        x = jax.random.normal(k_x, (B, N, DIM), dtype=jnp.float32)
        w_qkv = jax.random.normal(k_qkv, (DIM, 3 * DIM), dtype=jnp.float32) * (1.0 / np.sqrt(DIM))
        proj_matrix = jax.random.normal(k_proj, (HEADS, HEAD_DIM, FEAT), dtype=jnp.float32) * (1.0 / np.sqrt(HEAD_DIM))
        w_out = jax.random.normal(k_wo, (DIM, DIM), dtype=jnp.float32) * (1.0 / np.sqrt(DIM))
        b_out = jax.random.normal(k_bo, (DIM,), dtype=jnp.float32) * 0.01
        return {'x': x, 'w_qkv': w_qkv, 'proj_matrix': proj_matrix, 'w_out': w_out, 'b_out': b_out}
    _L0_attn_all = _L0_attn_setup()
    _L0_attn_in = {k: v for k, v in _L0_attn_all.items() if k in ('w_qkv', 'proj_matrix', 'w_out', 'b_out')}
    del _L0_attn_all

    def _L0_xattn_setup():
        import jax, jax.numpy as jnp
        import numpy as np
        import math
        B, S, D, H = (2, 256, 128, 16)
        DK = D // H
        key = jax.random.key(seed)
        ks = jax.random.split(key, 11)
        s = 1.0 / math.sqrt(D)
        return {'q': jax.random.normal(ks[0], (B, S, D), jnp.float32), 'k': jax.random.normal(ks[1], (B, S, D), jnp.float32), 'v': jax.random.normal(ks[2], (B, S, D), jnp.float32), 'Wq': jax.random.normal(ks[3], (D, D), jnp.float32) * s, 'bq': jax.random.normal(ks[4], (D,), jnp.float32) * s, 'Wk': jax.random.normal(ks[5], (D, D), jnp.float32) * s, 'bk': jax.random.normal(ks[6], (D,), jnp.float32) * s, 'Wv': jax.random.normal(ks[7], (D, D), jnp.float32) * s, 'bv': jax.random.normal(ks[8], (D,), jnp.float32) * s, 'Wo': jax.random.normal(ks[9], (D, D), jnp.float32) * s, 'bo': jax.random.normal(ks[10], (D,), jnp.float32) * s}
    _L0_xattn_all = _L0_xattn_setup()
    _L0_xattn_in = {k: v for k, v in _L0_xattn_all.items() if k in ('Wq', 'bq', 'Wk', 'bk', 'Wv', 'bv', 'Wo', 'bo')}
    del _L0_xattn_all

    def _L0_ffn_setup():
        import jax, jax.numpy as jnp
        import numpy as np
        B, S, D_MODEL, D_FF = (4, 256, 128, 512)

        def _quantum_transform(hidden, theta, w_real, w_imag):
            imag = w_imag * jnp.sin(theta + hidden * 0.1)
            quantum_phase = jnp.cos(theta) * w_real + jnp.sin(theta) * w_imag
            return hidden + quantum_phase * imag * 0.1
        key = jax.random.key(seed)
        ks = jax.random.split(key, 8)
        return {'x': jax.random.normal(ks[0], (B, S, D_MODEL), dtype=jnp.float32), 'W1': jax.random.normal(ks[1], (D_MODEL, D_FF), dtype=jnp.float32) * (1.0 / np.sqrt(D_MODEL)), 'b1': jnp.zeros((D_FF,), dtype=jnp.float32), 'quantum_phases': jax.random.normal(ks[2], (D_FF,), dtype=jnp.float32) * (2.0 * np.pi), 'quantum_weights_real': jax.random.normal(ks[3], (D_FF,), dtype=jnp.float32) * 0.1, 'quantum_weights_imag': jax.random.normal(ks[4], (D_FF,), dtype=jnp.float32) * 0.1, 'W2': jax.random.normal(ks[5], (D_FF, D_MODEL), dtype=jnp.float32) * (1.0 / np.sqrt(D_FF)), 'b2': jnp.zeros((D_MODEL,), dtype=jnp.float32)}
    _L0_ffn_all = _L0_ffn_setup()
    _L0_ffn_in = {k: v for k, v in _L0_ffn_all.items() if k in ('W1', 'b1', 'quantum_phases', 'quantum_weights_real', 'quantum_weights_imag', 'W2', 'b2')}
    del _L0_ffn_all
    return {'x': x, 'ctx_1024': ctx_1024, 'L0_attn_w_qkv': _L0_attn_in['w_qkv'], 'L0_attn_proj_matrix': _L0_attn_in['proj_matrix'], 'L0_attn_w_out': _L0_attn_in['w_out'], 'L0_attn_b_out': _L0_attn_in['b_out'], 'L0_xattn_Wq': _L0_xattn_in['Wq'], 'L0_xattn_bq': _L0_xattn_in['bq'], 'L0_xattn_Wk': _L0_xattn_in['Wk'], 'L0_xattn_bk': _L0_xattn_in['bk'], 'L0_xattn_Wv': _L0_xattn_in['Wv'], 'L0_xattn_bv': _L0_xattn_in['bv'], 'L0_xattn_Wo': _L0_xattn_in['Wo'], 'L0_xattn_bo': _L0_xattn_in['bo'], 'L0_ffn_W1': _L0_ffn_in['W1'], 'L0_ffn_b1': _L0_ffn_in['b1'], 'L0_ffn_quantum_phases': _L0_ffn_in['quantum_phases'], 'L0_ffn_quantum_weights_real': _L0_ffn_in['quantum_weights_real'], 'L0_ffn_quantum_weights_imag': _L0_ffn_in['quantum_weights_imag'], 'L0_ffn_W2': _L0_ffn_in['W2'], 'L0_ffn_b2': _L0_ffn_in['b2']}

def reference(x, ctx_1024, L0_attn_w_qkv, L0_attn_proj_matrix, L0_attn_w_out, L0_attn_b_out, L0_xattn_Wq, L0_xattn_bq, L0_xattn_Wk, L0_xattn_bk, L0_xattn_Wv, L0_xattn_bv, L0_xattn_Wo, L0_xattn_bo, L0_ffn_W1, L0_ffn_b1, L0_ffn_quantum_phases, L0_ffn_quantum_weights_real, L0_ffn_quantum_weights_imag, L0_ffn_W2, L0_ffn_b2):
    import jax
    import jax.numpy as jnp

    def _L0_attn_ref(x, w_qkv, proj_matrix, w_out, b_out):
        import jax, jax.numpy as jnp
        import numpy as np
        DIM = 128
        HEADS = 16
        HEAD_DIM = DIM // HEADS
        FEAT = 32
        B, N = (4, 512)

        def _elu1(x):
            return jnp.where(x > 0, x + 1.0, jnp.exp(x))
        b, n, d = x.shape
        h, hd = (HEADS, HEAD_DIM)
        qkv = x @ w_qkv
        q, k, v = jnp.split(qkv, 3, axis=-1)
        to_heads = lambda t: t.reshape(b, n, h, hd).transpose(0, 2, 1, 3)
        q, k, v = (to_heads(q), to_heads(k), to_heads(v))
        q_proj = _elu1(jnp.einsum('bhnd,hdf->bhnf', q, proj_matrix))
        k_proj = _elu1(jnp.einsum('bhnd,hdf->bhnf', k, proj_matrix))
        kv = jnp.einsum('bhnf,bhnd->bhfd', k_proj, v)
        attn = jnp.einsum('bhnf,bhfd->bhnd', q_proj, kv)
        k_sum = k_proj.sum(axis=2)
        z = 1.0 / (jnp.einsum('bhnf,bhf->bhn', q_proj, k_sum) + 1e-08)
        attn = attn * z[..., None]
        out = attn.transpose(0, 2, 1, 3).reshape(b, n, d)
        return out @ w_out + b_out

    def _L0_xattn_ref(q, k, v, Wq, bq, Wk, bk, Wv, bv, Wo, bo):
        import jax, jax.numpy as jnp
        import numpy as np
        import math
        B, S, D, H = (2, 256, 128, 16)
        DK = D // H
        bs = q.shape[0]
        qh = (q @ Wq.T + bq).reshape(bs, -1, H, DK).transpose(0, 2, 1, 3)
        kh = (k @ Wk.T + bk).reshape(bs, -1, H, DK).transpose(0, 2, 1, 3)
        vh = (v @ Wv.T + bv).reshape(bs, -1, H, DK).transpose(0, 2, 1, 3)
        scores = jnp.einsum('bhqd,bhkd->bhqk', qh, kh) / math.sqrt(DK)
        attn = jax.nn.softmax(scores, axis=-1)
        out = jnp.einsum('bhqk,bhkd->bhqd', attn, vh)
        concat = out.transpose(0, 2, 1, 3).reshape(bs, -1, D)
        return concat @ Wo.T + bo

    def _L0_ffn_ref(x, W1, b1, quantum_phases, quantum_weights_real, quantum_weights_imag, W2, b2):
        import jax, jax.numpy as jnp
        import numpy as np
        B, S, D_MODEL, D_FF = (4, 256, 128, 512)

        def _quantum_transform(hidden, theta, w_real, w_imag):
            imag = w_imag * jnp.sin(theta + hidden * 0.1)
            quantum_phase = jnp.cos(theta) * w_real + jnp.sin(theta) * w_imag
            return hidden + quantum_phase * imag * 0.1
        hidden = jnp.einsum('bsd,df->bsf', x, W1) + b1
        q = _quantum_transform(hidden, quantum_phases, quantum_weights_real, quantum_weights_imag)
        act = jax.nn.relu(q)
        return jnp.einsum('bsf,fd->bsd', act, W2) + b2
    x = _layernorm(x + _L0_attn_ref(x, L0_attn_w_qkv, L0_attn_proj_matrix, L0_attn_w_out, L0_attn_b_out), axis=-1)
    x = _layernorm(x + _L0_xattn_ref(x, ctx_1024, ctx_1024, L0_xattn_Wq, L0_xattn_bq, L0_xattn_Wk, L0_xattn_bk, L0_xattn_Wv, L0_xattn_bv, L0_xattn_Wo, L0_xattn_bo), axis=-1)
    x = _layernorm(x + _L0_ffn_ref(x, L0_ffn_W1, L0_ffn_b1, L0_ffn_quantum_phases, L0_ffn_quantum_weights_real, L0_ffn_quantum_weights_imag, L0_ffn_W2, L0_ffn_b2), axis=-1)
    return x

_drawn_inputs = setup_inputs


def setup_inputs(seed=0):
    import zlib

    import numpy as np

    out = dict(_drawn_inputs(seed))
    spreads = {'L0_ffn_b1': (0.0, 0.1), 'L0_ffn_b2': (0.0, 0.1)}
    factors = {'L0_attn_proj_matrix': 3.079,
     'L0_attn_b_out': 6.353,
     'L0_xattn_bq': 3.242,
     'L0_xattn_bk': 64.0,
     'L0_ffn_quantum_phases': 8.0,
     'L0_ffn_quantum_weights_real': 34.796,
     'L0_ffn_quantum_weights_imag': 8.0}
    for name, (base, spread) in spreads.items():
        noise = np.random.default_rng([zlib.crc32(name.encode()), seed]).standard_normal(out[name].shape)
        drawn = base * np.exp(spread * noise) if base else spread * noise
        out[name] = jnp.asarray(drawn.astype(out[name].dtype))
    for name, factor in factors.items():
        out[name] = (out[name] * factor).astype(out[name].dtype)
    return out
```

```python
from contextlib import ExitStack

import numpy as np

import concourse.bass as bass
from concourse import mybir

F32 = mybir.dt.float32
F16 = mybir.dt.float16
ALU = mybir.AluOpType
ACT = mybir.ActivationFunctionType
AX = mybir.AxisListType

P = 128
B, N, D = 32, 56, 128
S = 1500
H, HD = 16, 8
FEAT = 32
FF = 512
SLOT = 64
QUADS = B // 8
QT = 8 * SLOT
G = 4
GC = 4 * N
HQ = H * N
KP = 125
KT = S // KP
KC = 3
CH = S // KC
MB = HQ // P
NM = MB * KC
ROWS = 97
SHIFT = 64.0
PBUF = 3
RING = 3
KVW = 36
SCALE = float(HD) ** -0.5
EPS = 1e-5
ROUND = 1.5 * 2.0 ** 23
INV2PI = float(1.0 / (2.0 * np.pi))
TWO_PI_BELOW = 6.283185
C1 = 6.28125
C2 = 0.0019350051879882812
C3 = float(2.0 * np.pi - C1 - C2)

PACK = {}
_at = 0
for _name, _w in (("ident", P), ("wqT", P), ("wkT", P), ("wv", P), ("proj", H * FEAT), ("w_out", P),
                  ("WqT", P), ("WkT", P), ("WvT", P), ("WoT", P), ("WoSlots", 4 * P), ("selA", P),
                  ("selB", P), ("maskKV", 8 * KVW), ("maskQ", 4), ("maskM", H), ("W1", FF), ("W2", FF),
                  ("bq", 1), ("bk", 1), ("bv", 1), ("b1", 4), ("theta", 4), ("wr", 4), ("wi", 4),
                  ("rows", 3 * P)):
    PACK[_name] = (_at, _w)
    _at += _w
PACKW = _at


def settle(engine, counter):
    engine.nop().then_inc(counter, 1)


def wait_past(engine, semaphore, count):
    if not isinstance(count, int) or count > 0:
        engine.wait_ge(semaphore, count)


def unit_plan():
    steps = [[] for _ in range(KT)]
    m = 0
    for t in range(9):
        for _ in range(3 if t % 3 == 0 else 2):
            steps[t].append(("M", m))
            m += 1
    for c, t in enumerate((3, 5, 7)):
        steps[t].append(("V", c))
    steps[8] += [("T", 0)]
    steps[9] += [("T", 1), ("T", 2)]
    return steps


def ring_slots():
    order = [unit for step in unit_plan() for unit in step] + [("K", c) for c in range(KC)]
    return {unit: k % RING for k, unit in enumerate(order)}


def build(nc, ctx_dram, x_dram, pack_dram, out_dram):
    with ExitStack() as stack:
        def sb(name, shape, dt=F32):
            return stack.enter_context(nc.sbuf_tensor(name, shape, dt))

        def sem(name):
            return stack.enter_context(nc.semaphore(name))

        pack = sb("pack", [P, PACKW])

        def w(name, rows=slice(0, P)):
            at, width = PACK[name]
            return pack[rows, at:at + width]

        ident = w("ident")
        wslots = w("WoSlots").rearrange("p (s n) -> p s n", s=4)
        row_at = PACK["rows"][0]
        b_out_row, bo_row, b2_row = (pack[0:1, row_at + i * P:row_at + (i + 1) * P] for i in range(3))
        ones = sb("ones", [P, P])
        eps = sb("eps", [P, 1])
        wqp = sb("wqp", [P, H * FEAT])
        wkp = sb("wkp", [P, H * FEAT])
        WkH, WkL = sb("WkH", [P, P], F16), sb("WkL", [P, P], F16)
        WvH, WvL = sb("WvH", [P, P], F16), sb("WvL", [P, P], F16)
        x_all = sb("x_all", [P, QUADS, 4 * D])
        qh = sb("qh", [P, B * SLOT], F16)
        q_stack = sb("q_stack", [96, G, B * SLOT], F16)
        u_bias = sb("u_bias", [P, 4])
        s_coef = sb("s_coef", [P, 4])
        theta_r = sb("theta_r", [P, 4])

        psum = stack.enter_context(nc.psum_tensor("psum", [P, 8, 512], F32))
        banks = [psum[:, i, :] for i in range(8)]

        linear_attention_block(nc, x_dram, pack_dram, locals())
        cross_attention_block(nc, ctx_dram, locals())
        ffn_block(nc, out_dram, locals())


def layernorm_steps(nc, dve, src, dst, stats, mv, std, rstd, sems, q):
    stats_done, var_ready, std_ready, rstd_ready, settled = sems
    for p in range(4):
        last = nc.vector.bn_stats(stats[:, p, :], src[:, p * D:(p + 1) * D])
    last.then_inc(stats_done, 1)
    dve.wait_ge(stats_done, q + 1)
    settle(dve, settled)
    for p in range(4):
        last = nc.vector.bn_aggr(mv[:, p, :], stats[:, p, :])
    last.then_inc(var_ready, 1)
    dve.wait_ge(std_ready, q + 1)
    nc.vector.reciprocal(rstd[:, :], std[:, :]).then_inc(rstd_ready, 1)
    dve.wait_ge(rstd_ready, q + 1)
    for p in range(4):
        last = nc.vector.tensor_scalar(dst[:, p * D:(p + 1) * D], src[:, p * D:(p + 1) * D],
                                       mv[:, p, 0:1], rstd[:, p:p + 1], ALU.subtract, ALU.mult)
    return last


def linear_attention_block(nc, x_dram, pack_dram, m):
    pack, w, ident, ones, eps = m["pack"], m["w"], m["ident"], m["ones"], m["eps"]
    wqp, wkp, wslots = m["wqp"], m["wkp"], m["wslots"]
    x_all, qh, q_stack, banks = m["x_all"], m["qh"], m["q_stack"], m["banks"]
    with ExitStack() as stack:
        def sb(name, shape, dt=F32):
            return stack.enter_context(nc.sbuf_tensor(name, shape, dt))

        def sem(name):
            return stack.enter_context(nc.semaphore(name))

        xq = sb("xq", [P, 4 * D])
        xT = sb("xT", [P, QT])
        e_buf = sb("e_buf", [P, 2, 512])
        kf = sb("kf", [P, 4, H * FEAT])
        qf = sb("qf", [P, G, QT])
        v_s = sb("v_s", [P, 4 * G, KVW])
        kvm = sb("kvm", [P, 2, 2, 8, KVW])
        den = sb("den", [P, 2, 8 * 4])
        rden = sb("rden", [P, 2, 8 * 4])
        attn = sb("attn", [P, 4 * D])
        aT = sb("aT", [P, QT])
        xr = sb("xr", [P, 4 * D])
        x1 = sb("x1", [P, 4 * D])
        x1T = sb("x1T", [P, QT])
        ql = sb("ql", [P, B * SLOT], F16)
        stats, mv = sb("stats", [P, 4, 6]), sb("mv", [P, 4, 2])
        std, rstd = sb("std", [P, 4]), sb("rstd", [P, 4])
        ang = sb("ang", [P, 8, 4])

        pack_loaded, zeroed, x_loaded = sem("pack_loaded"), sem("zeroed"), sem("x_loaded")
        fold_ps, fold_sb, split_hi, split_done = sem("fold_ps"), sem("fold_sb"), sem("split_hi"), sem("split_done")
        bias_ps, bias_done = sem("bias_ps"), sem("bias_done")
        c_step, sin_done, cos_in = sem("c_step"), sem("sin_done"), sem("cos_in")
        xT_ps, xT_sb = sem("xT_ps"), sem("xT_sb")
        feat_ps, feat_exp, feat_min, feat_done = sem("feat_ps"), sem("feat_exp"), sem("feat_min"), sem("feat_done")
        v_ps, v_sb = sem("v_ps"), sem("v_sb")
        kv_ps, kv_sb = sem("kv_ps"), sem("kv_sb")
        at_ps, den_done, rden_done, attn_done = sem("at_ps"), sem("den_done"), sem("rden_done"), sem("attn_done")
        aT_ps, aT_sb, y_ps, xr_done = sem("aT_ps"), sem("aT_sb"), sem("y_ps"), sem("xr_done")
        ln = sem("ln1_stats"), sem("ln1_var"), sem("ln1_std"), sem("ln1_rstd"), sem("ln1_settled")
        x1_done, x1_kept = sem("x1_done"), sem("x1_kept")
        x1T_ps, x1T_sb, q_ps, qh_done, ql_done = (sem("x1T_ps"), sem("x1T_sb"), sem("q_ps"), sem("qh_done"),
                                                  sem("ql_done"))
        stacked = sem("q_stacked")
        pool_settled, sp_settled = sem("pool_settled1"), sem("sp_settled1")
        x_view = x_dram.rearrange("(q p e) n d -> q e n p d", q=QUADS, e=2)
        mask_kv = w("maskKV").rearrange("p (e a c) -> p e a c", e=1, a=8).to_broadcast([P, 2, 8, KVW])
        psum, T2, Y2 = m["psum"], banks[6], banks[7]

        with nc.Block() as block:
            @block.sync
            def _(sp):
                sp.dma_start(pack[:, :], pack_dram).then_inc(pack_loaded, 16)
                sp.wait_ge(zeroed, 1)

                def quad(q):
                    wait_past(sp, xr_done, q)
                    settle(sp, sp_settled)
                    for e in range(2):
                        src = x_view[bass.ds(q, 1), e, :, :, :].rearrange("o n p d -> n (o p) d")
                        sp.dma_start(xq[SLOT * e:SLOT * e + N, :].rearrange("r (p d) -> r p d", p=4),
                                     src).then_inc(x_loaded, 16)

                quad(0)
                with sp.Fori(1, QUADS) as q:
                    quad(q)
                sp.wait_ge(qh_done, QUADS)
                sp.wait_ge(ql_done, QUADS)
                for c, part in enumerate((qh, ql, qh)):
                    for g in range(G):
                        sp.dma_start(q_stack[32 * c:32 * c + 32, g, :],
                                     part[32 * g:32 * g + 32, :]).then_inc(stacked, 16)
                sp.wait_ge(stacked, 16 * 12)

            @block.gpsimd
            def _(pool):
                pool.memset(xq[:, :], 0.0).then_inc(zeroed, 1)
                pool.memset(ones[:, :], 1.0).then_inc(zeroed, 1)
                pool.memset(v_s[:, :, :], 1.0).then_inc(zeroed, 1)
                pool.memset(eps[:, :], EPS).then_inc(zeroed, 1)

                def quad(q):
                    for u in range(8):
                        pool.wait_ge(feat_exp, q * 8 + u + 1)
                        settle(pool, pool_settled)
                        nc.gpsimd.tensor_scalar(e_buf[:, u % 2, :], e_buf[:, u % 2, :], 1.0, None,
                                                ALU.min).then_inc(feat_min, 1)
                    pool.wait_ge(x1_done, q + 1)
                    settle(pool, pool_settled)
                    nc.gpsimd.tensor_copy(x_all[:, bass.ds(q, 1), :].rearrange("p o n -> p (o n)"),
                                          x1[:, :]).then_inc(x1_kept, 1)

                quad(0)
                with pool.Fori(1, QUADS) as q:
                    quad(q)

            @block.scalar
            def _(act):
                for i, dst in enumerate((wqp, wkp)):
                    act.wait_ge(fold_ps, i + 1)
                    nc.scalar.copy(dst[:, :], banks[2 + i][:, :]).then_inc(fold_sb, 1)
                act.wait_ge(cos_in, 1)
                nc.scalar.activation(ang[:, 3:5, :], ang[:, 1:3, :], ACT.Sin,
                                     scale=TWO_PI_BELOW).then_inc(sin_done, 1)
                act.wait_ge(zeroed, 4)

                def quad(q):
                    act.wait_ge(xT_ps, q + 1)
                    nc.scalar.copy(xT[:, :], banks[0][:, :]).then_inc(xT_sb, 1)
                    for u in range(8):
                        act.wait_ge(feat_ps, q * 8 + u + 1)
                        wait_past(act, feat_done, q * 8 + u - 1)
                        nc.scalar.activation(e_buf[:, u % 2, :], banks[2 + u % 4][:, :],
                                             ACT.Exp).then_inc(feat_exp, 1)
                    act.wait_ge(v_ps, q + 1)
                    nc.scalar.copy(v_s[:, :, 0:32],
                                   banks[1][:, :].rearrange("p (a c) -> p a c", c=32)).then_inc(v_sb, 1)
                    act.wait_ge(aT_ps, q + 1)
                    nc.scalar.copy(aT[:, :], T2[:, :]).then_inc(aT_sb, 1)
                    act.wait_ge(ln[1], q + 1)
                    nc.scalar.activation(std[:, :], mv[:, :, 1], ACT.Sqrt,
                                         bias=eps[:, 0:1]).then_inc(ln[2], 1)
                    act.wait_ge(x1T_ps, q + 1)
                    nc.scalar.copy(x1T[:, :], banks[0][:, :]).then_inc(x1T_sb, 1)
                    act.wait_ge(q_ps, q + 1)
                    nc.scalar.activation(qh[:, bass.ds(q * QT, QT)], banks[1][:, :], ACT.Identity,
                                         bias=w("bq")).then_inc(qh_done, 1)

                quad(0)
                with act.Fori(1, QUADS) as q:
                    quad(q)

            @block.tensor
            def _(pe):
                pe.wait_ge(pack_loaded, 16)
                for i, name in enumerate(("wqT", "wkT")):
                    nc.tensor.matmul(banks[2 + i][:, :], w(name), w("proj"), start=True,
                                     stop=True).then_inc(fold_ps, 1)
                nc.tensor.matmul(banks[4][0:1, 0:P], w("bv"), w("WoT"), start=True, stop=True).then_inc(bias_ps, 1)
                pe.wait_ge(fold_sb, 2)
                pe.wait_ge(bias_done, 1)
                pe.wait_ge(zeroed, 4)

                def quad(q):
                    pe.wait_ge(x_loaded, q * 32 + 32)
                    wait_past(pe, x1T_sb, q)
                    for p in range(4):
                        last = nc.tensor.transpose(banks[0][:, p * P:(p + 1) * P], xq[:, p * D:(p + 1) * D], ident)
                    last.then_inc(xT_ps, 1)
                    pe.wait_ge(xT_sb, q + 1)
                    wait_past(pe, ql_done, q)
                    for p in range(4):
                        last = nc.tensor.matmul(banks[1][:, p * P:(p + 1) * P], xT[:, p * P:(p + 1) * P], w("wv"),
                                                start=True, stop=True)
                    last.then_inc(v_ps, 1)
                    for u in range(8):
                        wait_past(pe, feat_done, q * 8 + u - 3)
                        if u < 4:
                            mm = nc.tensor.matmul(banks[2 + u % 4][:, :], xT[:, u * P:(u + 1) * P], wkp[:, :],
                                                  start=True, stop=True)
                        else:
                            mm = nc.tensor.matmul(banks[2 + u % 4][:, :], wqp[:, (u - 4) * P:(u - 3) * P], xT[:, :],
                                                  start=True, stop=True)
                        mm.then_inc(feat_ps, 1)
                    pe.wait_ge(v_sb, q + 1)
                    wait_past(pe, aT_sb, q)
                    wait_past(pe, xr_done, q)
                    for i in range(2):
                        pe.wait_ge(feat_done, q * 8 + 2 * i + 2)
                        wait_past(pe, kv_sb, q * 2 + i)
                        for p in (2 * i, 2 * i + 1):
                            for e in range(2):
                                rows = slice(SLOT * e, SLOT * e + N)
                                for g in range(G):
                                    at = (4 * (p % 2) + g) * KVW
                                    last = nc.tensor.matmul(banks[6 + e][:, at:at + KVW],
                                                            kf[rows, p, g * P:(g + 1) * P],
                                                            v_s[rows, p * G + g, :], start=True, stop=True)
                        last.then_inc(kv_ps, 1)
                    pe.wait_ge(feat_done, q * 8 + 8)
                    for p in range(4):
                        pe.wait_ge(kv_sb, q * 2 + p // 2 + 1)
                        for e in range(2):
                            for g in range(G):
                                at = (p % 2) * G * KVW + g * KVW
                                last = nc.tensor.matmul(banks[p // 2][SLOT * e:SLOT * e + SLOT, at:at + KVW],
                                                        qf[:, g, p * P + SLOT * e:p * P + SLOT * e + SLOT],
                                                        kvm[:, p // 2, e, 4 * (p % 2) + g, :], start=True, stop=True)
                        if p % 2:
                            last.then_inc(at_ps, 1)
                    for p in range(4):
                        pe.wait_ge(attn_done, q * 2 + p // 2 + 1)
                        last = nc.tensor.transpose(T2[:, p * P:(p + 1) * P], attn[:, p * D:(p + 1) * D], ident)
                    last.then_inc(aT_ps, 1)
                    pe.wait_ge(aT_sb, q + 1)
                    for p in range(4):
                        nc.tensor.matmul(Y2[:, p * P:(p + 1) * P], aT[:, p * P:(p + 1) * P], w("w_out"),
                                         start=True, stop=False)
                        last = nc.tensor.matmul(Y2[:, p * P:(p + 1) * P], ones[0:1, :], m["b_out_row"],
                                                start=False, stop=True)
                    last.then_inc(y_ps, 1)
                    for p in range(4):
                        pe.wait_ge(x1_done, q + 1)
                        last = nc.tensor.transpose(banks[0][:, p * P:(p + 1) * P], x1[:, p * D:(p + 1) * D], ident)
                    last.then_inc(x1T_ps, 1)
                    pe.wait_ge(x1T_sb, q + 1)
                    nc.tensor.matmul(banks[1][:, :], w("WqT"), x1T[:, :], start=True, stop=True).then_inc(q_ps, 1)

                quad(0)
                with pe.Fori(1, QUADS) as q:
                    quad(q)

            @block.vector
            def _(dve):
                dve.wait_ge(pack_loaded, 16)
                for name, hi in (("WkT", m["WkH"]), ("WvT", m["WvH"])):
                    nc.vector.tensor_copy(hi[:, :], w(name)).then_inc(split_hi, 1)
                dve.wait_ge(split_hi, 2)
                for name, hi, lo in (("WkT", m["WkH"], m["WkL"]), ("WvT", m["WvH"], m["WvL"])):
                    nc.vector.tensor_tensor(lo[:, :], w(name), hi[:, :], ALU.subtract).then_inc(split_done, 1)
                dve.wait_ge(bias_ps, 1)
                nc.vector.tensor_tensor(wslots[0:1, 0, :], banks[4][0:1, 0:P], m["bo_row"],
                                        ALU.add).then_inc(bias_done, 1)
                steps = [0]

                def chain(ins):
                    ins.then_inc(c_step, 1)
                    steps[0] += 1
                    dve.wait_ge(c_step, steps[0])

                theta, theta_r = w("theta"), m["theta_r"]
                n, f0, f1, sn, cs = (ang[:, i, :] for i in (0, 1, 2, 3, 4))
                chain(nc.vector.tensor_scalar(n, theta, INV2PI, None, ALU.mult))
                chain(nc.vector.tensor_scalar(n, n, ROUND, -ROUND, ALU.add, ALU.add))
                chain(nc.vector.scalar_tensor_tensor(theta_r[:, :], n, -C1, theta, ALU.mult, ALU.add))
                chain(nc.vector.scalar_tensor_tensor(theta_r[:, :], n, -C2, theta_r[:, :], ALU.mult, ALU.add))
                chain(nc.vector.scalar_tensor_tensor(theta_r[:, :], n, -C3, theta_r[:, :], ALU.mult, ALU.add))
                chain(nc.vector.tensor_scalar(f0, theta_r[:, :], INV2PI, None, ALU.mult))
                chain(nc.vector.scalar_tensor_tensor(m["u_bias"][:, :], w("b1"), 0.1 * INV2PI, f0, ALU.mult, ALU.add))
                chain(nc.vector.tensor_scalar(f0, f0, 0.5, -0.5, ALU.min, ALU.max))
                chain(nc.vector.tensor_scalar(f1, f0, 0.25, None, ALU.add))
                chain(nc.vector.tensor_scalar(n, f1, ROUND, -ROUND, ALU.add, ALU.add))
                nc.vector.tensor_tensor(f1, f1, n, ALU.subtract).then_inc(cos_in, 1)
                dve.wait_ge(sin_done, 1)
                chain(nc.vector.tensor_tensor(ang[:, 5, :], cs, w("wr"), ALU.mult))
                chain(nc.vector.tensor_tensor(ang[:, 6, :], sn, w("wi"), ALU.mult))
                chain(nc.vector.tensor_tensor(ang[:, 5, :], ang[:, 5, :], ang[:, 6, :], ALU.add))
                chain(nc.vector.scalar_tensor_tensor(m["s_coef"][:, :], ang[:, 5, :], 0.1, w("wi"),
                                                     ALU.mult, ALU.mult))
                dve.wait_ge(zeroed, 4)

                def quad(q):
                    for u in range(8):
                        dve.wait_ge(feat_min, q * 8 + u + 1)
                        dst = kf[:, u, :] if u < 4 else qf[:, u - 4, :]
                        nc.vector.scalar_tensor_tensor(dst, banks[2 + u % 4][:, :], 0.0, e_buf[:, u % 2, :],
                                                       ALU.max, ALU.add).then_inc(feat_done, 1)
                    for i in range(2):
                        dve.wait_ge(kv_ps, q * 2 + i + 1)
                        src = psum[:, 6:8, 0:8 * KVW].rearrange("p e (a c) -> p e a c", a=8)
                        nc.vector.tensor_tensor(kvm[:, i, :, :, :], src, mask_kv, ALU.mult).then_inc(kv_sb, 1)
                    for i in range(2):
                        dve.wait_ge(at_ps, q * 2 + i + 1)
                        at = banks[i][:, 0:8 * KVW].rearrange("p (a c) -> p a c", a=8)
                        nc.vector.tensor_scalar(den[:, i, :].rearrange("p (a h) -> p a h", a=8), at[:, :, 32:36],
                                                1e-8, None, ALU.add).then_inc(den_done, 1)
                        dve.wait_ge(den_done, q * 2 + i + 1)
                        nc.vector.reciprocal(rden[:, i, :], den[:, i, :]).then_inc(rden_done, 1)
                        dve.wait_ge(rden_done, q * 2 + i + 1)
                        r = rden[:, i, :].rearrange("p (a h o) -> p a h o", a=8, o=1).to_broadcast([P, 8, 4, HD])
                        nc.vector.tensor_tensor(
                            attn[:, i * 2 * D:(i + 1) * 2 * D].rearrange("p (a h d) -> p a h d", a=8, d=HD),
                            at[:, :, 0:32].rearrange("p a (h d) -> p a h d", d=HD), r,
                            ALU.mult).then_inc(attn_done, 1)
                    dve.wait_ge(y_ps, q + 1)
                    nc.vector.tensor_tensor(xr[:, :], Y2[:, :], xq[:, :], ALU.add).then_inc(xr_done, 1)
                    dve.wait_ge(xr_done, q + 1)
                    wait_past(dve, x1_kept, q)
                    layernorm_steps(nc, dve, xr, x1, stats, mv, std, rstd, ln, q).then_inc(x1_done, 1)
                    dve.wait_ge(qh_done, q + 1)
                    nc.vector.scalar_tensor_tensor(ql[:, bass.ds(q * QT, QT)], banks[1][:, :], w("bq"),
                                                   qh[:, bass.ds(q * QT, QT)], ALU.add,
                                                   ALU.subtract).then_inc(ql_done, 1)

                quad(0)
                with dve.Fori(1, QUADS) as q:
                    quad(q)
class RingView:
    def __init__(self, ring):
        self.ring, self.slots, self.prologue = ring, ring_slots(), False

    def __call__(self, kind, i):
        return self.ring[i % RING if self.prologue else self.slots[kind, i]]


def cross_attention_block(nc, ctx_dram, m):
    w, banks, x_all, qh, q_stack, wslots = (m[k] for k in ("w", "banks", "x_all", "qh", "q_stack", "wslots"))
    WkH, WkL, WvH, WvL = m["WkH"], m["WkL"], m["WvH"], m["WvL"]
    plan = unit_plan()
    TPB = 8
    with ExitStack() as stack:
        def sb(name, shape, dt=F32):
            return stack.enter_context(nc.sbuf_tensor(name, shape, dt))

        def sem(name):
            return stack.enter_context(nc.semaphore(name))

        c_in = sb("c_in", [P, 2, KT * D])
        c_hl = sb("c_hl", [P, 2 * KT, D], F16)
        cT = sb("cT", [P, 2 * KT, P], F16)
        kh = sb("kh", [P, S], F16)
        kl = sb("kl", [P, S], F16)
        k_stack = [sb(f"k_stack{i}", [P, G, S + 4], F16) for i in range(2)]
        q_diag = [sb(f"q_diag{i}", [P, HQ], F16) for i in range(2)]
        q_max = [sb(f"q_max{i}", [P, HQ], F16) for i in range(2)]
        v_ext = [sb(f"v_ext{i}", [P, KT, G, 48]) for i in range(2)]
        probs = sb("probs", [P, PBUF, HQ])
        mx = sb("mx", [P, NM])
        mrow = sb("mrow", [P, MB])
        m16 = sb("m16", [P, 32], F16)
        mT = sb("mT", [P, 32], F16)
        o_sb = sb("o_sb", [P, GC])
        r_sb = sb("r_sb", [P, GC])
        o_n = sb("o_n", [P, GC])

        c_loaded, c_hi, c_split = [sem("c_loaded0"), sem("c_loaded1")], sem("c_hi"), sem("c_split")
        ready = {k: sem(f"unit_{k}") for k in "TKVM"}
        cT_done, kh_done, kl_done, v_done, mx_done = (sem("cT_done"), sem("kh_done"), sem("kl_done"),
                                                      sem("v_done"), sem("mx_done"))
        m_fold, m_cast, m_ready, m_placed = sem("m_fold"), sem("m_cast"), sem("m_ready"), sem("m_placed")
        qd_ready, qm_ready, k_stacked = sem("qd_ready"), sem("qm_ready"), sem("k_stacked")
        s_ready, p_ready, pv_done = sem("s_ready"), sem("p_ready"), sem("pv_done")
        o_copied, r_ready, r_inv, o_ready, y_ready, y_added = (sem("o_copied"), sem("r_ready"), sem("r_inv"),
                                                               sem("o_ready"), sem("y_ready"), sem("y_added"))
        init = sem("init2")
        pool_settled, sp_settled = sem("pool_settled2"), sem("sp_settled2")
        INIT = 3 + 7
        ident16 = sb("ident16", [P, P], F16)
        scores = [m["psum"][:, 0:2, :], m["psum"][:, 2:4, :]]
        ring = banks[4:7]
        O = banks[7]
        PER = {"T": 3, "K": 3, "V": 3, "M": NM}
        DONE = {"T": cT_done, "K": kl_done, "V": v_done, "M": mx_done}
        maskQ = w("maskQ")
        maskM = w("maskM")

        def unit_freed(pe, kind, i, n):
            pe.wait_ge(DONE[kind], n * PER[kind] + i + 1)

        def last_three(n):
            return [("K", c, n) for c in range(KC)]

        with nc.Block() as block:
            @block.sync
            def _(sp):
                def load(n, buf):
                    src = ctx_dram[bass.ds(n, 1), :, :].rearrange("o (p t) d -> p (o t d)", t=KT)
                    sp.dma_start(c_in[0:KP, buf, :], src).then_inc(c_loaded[buf], 16)

                def stack_k(n, u):
                    sp.wait_ge(kl_done, (n + 1) * KC)
                    settle(sp, sp_settled)
                    for c, part in enumerate((kh, kh, kl)):
                        for g in range(G):
                            sp.dma_start(k_stack[u][32 * c:32 * c + 32, g, 0:S],
                                         part[32 * g:32 * g + 32, :]).then_inc(k_stacked, 16)

                def place_m(n, u):
                    sp.wait_ge(m_ready, n + 1)
                    settle(sp, sp_settled)
                    row = q_diag[u][96:97, :].rearrange("o (r q i) -> o r q i", q=4, i=32)
                    for quarter in range(4):
                        sp.dma_start(row[:, :, quarter, :],
                                     mT[32 * quarter:32 * quarter + MB, :]).then_inc(m_placed, 16)

                load(0, 0)
                load(1, 1)
                sp.wait_ge(init, INIT)
                stack_k(0, 0)
                sp.wait_ge(c_split, 1)
                load(2, 0)
                sp.wait_ge(c_split, 2)
                load(3, 1)
                place_m(0, 0)

                def body(b, u, stage2, load4):
                    if load4:
                        sp.wait_ge(c_split, b + 3)
                        settle(sp, sp_settled)
                        load(b + 4, u)
                    if stage2:
                        wait_past(sp, s_ready, b * KT)
                        settle(sp, sp_settled)
                        stack_k(b + 1, 1 - u)
                        place_m(b + 1, 1 - u)

                for b in range(2):
                    body(b, b, True, True)
                with sp.Fori(1, (B - 4) // 2) as i:
                    for u in range(2):
                        body(i * 2 + u, u, True, True)
                for b in range(B - 4, B):
                    body(b, b % 2, b + 1 < B, b + 4 < B)

            @block.gpsimd
            def _(pool):
                for t in v_ext:
                    pool.memset(t[:, :, :, :], 1.0).then_inc(init, 1)
                pool.memset(m16[:, :], 0.0).then_inc(init, 1)

                def split(n, buf, half):
                    pool.wait_ge(c_loaded[buf], half * 16 + 16)
                    settle(pool, pool_settled)
                    src = c_in[0:KP, buf, :].rearrange("p (t d) -> p t d", t=KT)
                    nc.gpsimd.tensor_copy(c_hl[0:KP, 0:KT, :], src).then_inc(c_hi, 1)
                    pool.wait_ge(c_hi, n + 1)
                    nc.gpsimd.tensor_tensor(c_hl[0:KP, KT:2 * KT, :], src, c_hl[0:KP, 0:KT, :],
                                            ALU.subtract).then_inc(c_split, 1)

                def diag_q(n, u):
                    q = q_stack[0:96, :, bass.ds(n * SLOT, N)].rearrange("p g (o n) -> p g o n", o=1)
                    nc.gpsimd.tensor_tensor(
                        q_diag[u][0:96, :].rearrange("p (g h n) -> p g h n", g=G, h=4),
                        q.to_broadcast([96, G, 4, N]),
                        maskQ[0:96, :].rearrange("p (o h e) -> p o h e", o=1, e=1).to_broadcast([96, G, 4, N]),
                        ALU.mult).then_inc(qd_ready, 1)

                def max_q(n, u):
                    q = qh[:, bass.ds(n * SLOT, N)].rearrange("p (o n) -> p o n", o=1)
                    nc.gpsimd.tensor_tensor(
                        q_max[u][:, :].rearrange("p (h n) -> p h n", h=H), q.to_broadcast([P, H, N]),
                        maskM.rearrange("p (h o) -> p h o", o=1).to_broadcast([P, H, N]),
                        ALU.mult).then_inc(qm_ready, 1)

                pool.wait_ge(init, INIT)
                split(0, 0, 0)
                max_q(0, 0)
                diag_q(0, 0)
                pool.wait_ge(ready["T"], 3)
                split(1, 1, 0)
                max_q(1, 1)
                pool.wait_ge(ready["T"], 6)
                split(2, 0, 1)

                def body(b, pair, u, s1, s2, s3):
                    if s2:
                        wait_past(pool, s_ready, b * KT)
                        diag_q(b + 1, 1 - u)
                    if s1:
                        pool.wait_ge(ready["M"], (b + 1) * NM)
                        max_q(b + 2, u)
                    if s3:
                        pool.wait_ge(ready["T"], b * 3 + 9)
                        split(b + 3, 1 - u, pair + 1 + u)

                for b in range(2):
                    body(b, 0, b, True, True, True)
                with pool.Fori(1, (B - 4) // 2) as i:
                    for u in range(2):
                        body(i * 2 + u, i, u, True, True, True)
                for b in range(B - 4, B):
                    body(b, b // 2, b % 2, b + 2 < B, b + 1 < B, b + 3 < B)

            @block.tensor
            def _(pe):
                def unit(kind, i, n, u, slot, before):
                    if before is not None:
                        unit_freed(pe, *before)
                    bank = ring[slot]
                    if kind == "T":
                        if i == 0:
                            pe.wait_ge(c_split, n + 1)
                        out = bank[:, :].bitcast(F16).rearrange("p (t k) -> p t k", t=TPB)
                        for j in range(TPB):
                            last = nc.tensor.transpose(out[:, j, :], c_hl[:, i * TPB + j, :], ident16[:, :])
                    elif kind == "K":
                        if i == 0:
                            pe.wait_ge(cT_done, n * 3 + 3)
                        for k, (wt, part) in enumerate(((WkH, 0), (WkH, KT), (WkL, 0))):
                            last = nc.tensor.matmul(bank[:, 0:CH], wt[:, :],
                                                    cT[:, part + 4 * i:part + 4 * i + 4, 0:KP],
                                                    start=(k == 0), stop=(k == 2))
                    elif kind == "V":
                        for j in range(4):
                            t = 4 * i + j
                            for k, (part, wt) in enumerate(((0, WvH), (KT, WvH), (0, WvL))):
                                last = nc.tensor.matmul(bank[:, j * P:(j + 1) * P], cT[:, part + t, :], wt[:, :],
                                                        start=(k == 0), stop=(k == 2))
                    else:
                        r, c = divmod(i, KC)
                        if i == 0:
                            pe.wait_ge(kh_done, n * KC + KC)
                            pe.wait_ge(qm_ready, n + 1)
                        last = nc.tensor.matmul(bank[:, 0:CH], q_max[u][:, r * P:(r + 1) * P],
                                                kh[:, c * CH:(c + 1) * CH], start=True, stop=True)
                    last.then_inc(ready[kind], 1)

                class Ring:
                    def __init__(self, held):
                        self.held, self.k = list(held), 0

                    def go(self, kind, i, n, u):
                        slot = self.k % RING
                        unit(kind, i, n, u, slot, self.held[slot])
                        self.held[slot] = (kind, i, n)
                        self.k += 1

                def score(b, t, u):
                    if t == 0:
                        pe.wait_ge(k_stacked, (b + 1) * 16 * 12)
                        pe.wait_ge(qd_ready, b + 1)
                        pe.wait_ge(m_placed, (b + 1) * 64)
                    wait_past(pe, p_ready, b * KT + t - 1)
                    for g in range(G):
                        last = nc.tensor.matmul(scores[t % 2][:, g // 2, (g % 2) * GC:(g % 2 + 1) * GC],
                                                k_stack[u][0:ROWS, g, t * KP:t * KP + P],
                                                q_diag[u][0:ROWS, g * GC:(g + 1) * GC], start=True, stop=True)
                    last.then_inc(s_ready, 1)

                def pv(b, t, u):
                    if t == 0:
                        pe.wait_ge(v_done, b * 3 + 3)
                        wait_past(pe, y_added, b)
                    pe.wait_ge(p_ready, b * KT + t + 1)
                    for j in range(G):
                        at = j * GC
                        nc.tensor.matmul(O[32 * j:32 * j + 32, 0:3 * N], v_ext[u][0:KP, t, j, 0:32],
                                         probs[0:KP, t % PBUF, at:at + 3 * N], start=(t == 0), stop=(t == KT - 1),
                                         skip_group_check=True)
                    for j in range(G):
                        at = j * GC
                        last = nc.tensor.matmul(O[32 * j:32 * j + 16, 3 * N:GC], v_ext[u][0:KP, t, j, 32:48],
                                                probs[0:KP, t % PBUF, at + 3 * N:at + GC], start=False,
                                                stop=(t == KT - 1), skip_group_check=True)
                    last.then_inc(pv_done, 1)

                def body(b, u, s1, s2):
                    r = Ring(last_three(b + 1))
                    for t in range(KT):
                        score(b, t, u)
                        for kind, i in plan[t]:
                            if kind in "MV" and s2:
                                r.go(kind, i, b + 1, 1 - u)
                            if kind == "T" and s1:
                                r.go(kind, i, b + 2, u)
                        if t:
                            pv(b, t - 1, u)
                    if s1:
                        r.go("K", 0, b + 2, u)
                    pv(b, KT - 1, u)
                    if s1:
                        r.go("K", 1, b + 2, u)
                    pe.wait_ge(o_copied, b + 1)
                    nc.tensor.matmul(O[:, 256:256 + 3 * N], w("selA"), o_sb[:, 0:3 * N], start=True, stop=True)
                    nc.tensor.matmul(O[:, 256 + 3 * N:256 + GC], w("selB"), o_sb[:, 3 * N:GC], start=True,
                                     stop=True).then_inc(r_ready, 1)
                    if s1:
                        r.go("K", 2, b + 2, u)
                    pe.wait_ge(o_ready, b + 1)
                    for s in range(4):
                        last = nc.tensor.matmul(O[SLOT * u:SLOT * u + N, 0:D], o_n[:, s * N:(s + 1) * N],
                                                wslots[:, s, :], start=(s == 0), stop=(s == 3))
                    last.then_inc(y_ready, 1)

                pe.wait_ge(init, INIT)
                r = Ring([None] * RING)
                for kind, count, n in (("T", 3, 0), ("K", 3, 0), ("V", 3, 0), ("M", NM, 0), ("T", 3, 1), ("K", 3, 1)):
                    for i in range(count):
                        r.go(kind, i, n, n % 2)
                for b in range(2):
                    body(b, b % 2, True, True)
                with pe.Fori(1, B // 2 - 1) as i:
                    for u in range(2):
                        body(i * 2 + u, u, True, True)
                for b in range(B - 2, B):
                    body(b, b % 2, b + 2 < B, b + 1 < B)

            @block.scalar
            def _(act):
                def exp(b, t):
                    act.wait_ge(s_ready, b * KT + t + 1)
                    wait_past(act, pv_done, b * KT + t - PBUF + 1)
                    src = scores[t % 2][0:KP, :, 0:2 * GC]
                    nc.scalar.activation(probs[0:KP, t % PBUF, :].rearrange("p (a c) -> p a c", a=2), src,
                                         ACT.Exp, scale=SCALE).then_inc(p_ready, 1)

                def v_copy(n, i, u):
                    act.wait_ge(ready["V"], n * 3 + i + 1)
                    nc.scalar.copy(v_ext[u][0:KP, 4 * i:4 * i + 4, :, 8:40],
                                   ring_at("V", i)[0:KP, :].rearrange("p (t j c) -> p t j c", t=4, j=G)
                                   ).then_inc(v_done, 1)

                def k_hi(n, i):
                    act.wait_ge(ready["K"], n * 3 + i + 1)
                    if i == 0:
                        wait_past(act, ready["M"], n * NM)
                        wait_past(act, k_stacked, n * 192)
                    nc.scalar.activation(kh[:, i * CH:(i + 1) * CH], ring_at("K", i)[:, 0:CH], ACT.Identity,
                                         bias=w("bk")).then_inc(kh_done, 1)

                ring_at = RingView(ring)
                act.wait_ge(init, INIT)
                ring_at.prologue = True
                for i in range(3):
                    k_hi(0, i)
                for i in range(3):
                    v_copy(0, i, 0)
                for i in range(3):
                    k_hi(1, i)
                ring_at.prologue = False

                def body(b, u, s1, s2):
                    for t in range(KT):
                        exp(b, t)
                        for kind, i in plan[t]:
                            if kind == "V" and s2:
                                v_copy(b + 1, i, 1 - u)
                    if s1:
                        for i in range(3):
                            k_hi(b + 2, i)

                for b in range(2):
                    body(b, b % 2, True, True)
                with act.Fori(1, B // 2 - 1) as i:
                    for u in range(2):
                        body(i * 2 + u, u, True, True)
                for b in range(B - 2, B):
                    body(b, b % 2, b + 2 < B, b + 1 < B)

            @block.vector
            def _(dve):
                nc.vector.memset(c_hl[96:P, :, :], 0.0).then_inc(init, 1)
                for t in k_stack:
                    nc.vector.memset(t[96:97, :, :], SHIFT).then_inc(init, 1)
                    nc.vector.memset(t[0:96, :, S:S + 4], 0.0).then_inc(init, 1)
                nc.vector.memset(O[:, :], 0.0).then_inc(init, 1)
                nc.vector.tensor_copy(ident16[:, :], m["ident"]).then_inc(init, 1)
                dve.wait_ge(init, INIT)
                ring_at = RingView(ring)

                def t_copy(n, i):
                    dve.wait_ge(ready["T"], n * 3 + i + 1)
                    if i == 0:
                        wait_past(dve, ready["V"], n * 3)
                        wait_past(dve, ready["K"], n * 3)
                    nc.vector.tensor_copy(cT[:, i * TPB:(i + 1) * TPB, :],
                                          ring_at("T", i)[:, :].bitcast(F16).rearrange("p (t k) -> p t k", t=TPB)
                                          ).then_inc(cT_done, 1)

                def k_lo(n, i):
                    dve.wait_ge(kh_done, n * 3 + i + 1)
                    if i == 0:
                        wait_past(dve, k_stacked, n * 192)
                    nc.vector.scalar_tensor_tensor(kl[:, i * CH:(i + 1) * CH], ring_at("K", i)[:, 0:CH], w("bk"),
                                                   kh[:, i * CH:(i + 1) * CH], ALU.add,
                                                   ALU.subtract).then_inc(kl_done, 1)

                def m_max(n, i):
                    dve.wait_ge(ready["M"], n * NM + i + 1)
                    if i == 0:
                        wait_past(dve, m_fold, n)
                    nc.vector.tensor_reduce(mx[:, i:i + 1], ring_at("M", i)[:, 0:CH], AX.X,
                                            ALU.max).then_inc(mx_done, 1)

                def m_row(n):
                    dve.wait_ge(mx_done, (n + 1) * NM)
                    nc.vector.tensor_reduce(mrow[:, :], mx[:, :].rearrange("p (r c) -> p r c", c=KC), AX.X,
                                            ALU.max).then_inc(m_fold, 1)
                    dve.wait_ge(m_fold, n + 1)
                    nc.vector.tensor_scalar(m16[:, 0:MB], mrow[:, :], -1.0 / SHIFT, None,
                                            ALU.mult).then_inc(m_cast, 1)
                    dve.wait_ge(m_cast, n + 1)
                    wait_past(dve, m_placed, n * 64)
                    nc.vector.transpose(mT[:, :], m16[:, :]).then_inc(m_ready, 1)

                ring_at.prologue = True
                for i in range(3):
                    t_copy(0, i)
                for i in range(3):
                    k_lo(0, i)
                for i in range(NM):
                    m_max(0, i)
                m_row(0)
                for i in range(3):
                    t_copy(1, i)
                for i in range(3):
                    k_lo(1, i)
                ring_at.prologue = False

                def body(b, pair, u, s1, s2):
                    for t in range(KT):
                        for kind, i in plan[t]:
                            if kind == "M" and s2:
                                m_max(b + 1, i)
                                if i == NM - 1:
                                    m_row(b + 1)
                            if kind == "T" and s1:
                                t_copy(b + 2, i)
                    if s1:
                        k_lo(b + 2, 0)
                    dve.wait_ge(pv_done, b * KT + KT)
                    nc.vector.tensor_copy(o_sb[:, :], O[:, 0:GC]).then_inc(o_copied, 1)
                    if s1:
                        k_lo(b + 2, 1)
                    dve.wait_ge(r_ready, b + 1)
                    nc.vector.reciprocal(r_sb[:, :], O[:, 256:256 + GC]).then_inc(r_inv, 1)
                    dve.wait_ge(r_inv, b + 1)
                    nc.vector.tensor_tensor(o_n[:, :], o_sb[:, :], r_sb[:, :], ALU.mult).then_inc(o_ready, 1)
                    if s1:
                        k_lo(b + 2, 2)
                    dve.wait_ge(y_ready, b + 1)
                    rows = slice(SLOT * u, SLOT * u + N)
                    x_pairs = x_all[rows, :, :].rearrange("p q (a d) -> p (q a) d", a=4)
                    xs = x_pairs[:, bass.ds(pair, 1), :].rearrange("p o d -> p (o d)")
                    nc.vector.tensor_tensor(xs, O[rows, 0:D], xs, ALU.add).then_inc(y_added, 1)

                for b in range(2):
                    body(b, 0, b, True, True)
                with dve.Fori(1, B // 2 - 1) as i:
                    for u in range(2):
                        body(i * 2 + u, i, u, True, True)
                for b in range(B - 2, B):
                    body(b, b // 2, b % 2, b + 2 < B, b + 1 < B)


def ffn_block(nc, out_dram, m):
    w, banks, ident, ones, eps, x_all = (m[k] for k in ("w", "banks", "ident", "ones", "eps", "x_all"))
    with ExitStack() as stack:
        def sb(name, shape, dt=F32):
            return stack.enter_context(nc.sbuf_tensor(name, shape, dt))

        def sem(name):
            return stack.enter_context(nc.semaphore(name))

        xs = sb("xs", [P, 4 * D])
        x2 = sb("x2", [P, 4 * D])
        x2T = sb("x2T", [P, QT])
        turns = sb("turns", [P, 2, QT])
        whole = sb("whole", [P, 2, QT])
        frac = sb("frac", [P, 2, QT])
        sine = sb("sine", [P, 2, QT])
        z = sb("z", [P, 2, QT])
        hid = sb("hid", [P, G, QT])
        y = sb("y", [P, 4 * D])
        out_t = sb("out_t", [P, 4 * D])
        stats = [sb(f"stats{i}", [P, 4, 6]) for i in (2, 3)]
        mv = [sb(f"mv{i}", [P, 4, 2]) for i in (2, 3)]
        std = [sb(f"std{i}", [P, 4]) for i in (2, 3)]
        rstd = [sb(f"rstd{i}", [P, 4]) for i in (2, 3)]
        xs_ready, x2_done, x2T_ps, x2T_sb, h_ps = (sem("xs_ready"), sem("x2_done"), sem("x2T_ps"), sem("x2T_sb"),
                                                   sem("h_ps"))
        turns_ready, whole_ready, frac_ready, sine_ready = (sem("turns_ready"), sem("whole_ready"),
                                                            sem("frac_ready"), sem("sine_ready"))
        pool_settled, sp_settled = sem("pool_settled3"), sem("sp_settled3")
        z_ready, hid_ready, f_ps, y_done, out_ready, stored = (sem("z_ready"), sem("hid_ready"), sem("f_ps"),
                                                               sem("y_done"), sem("out_ready"), sem("stored"))
        ln2 = sem("ln2_stats"), sem("ln2_var"), sem("ln2_std"), sem("ln2_rstd"), sem("ln2_settled")
        ln3 = sem("ln3_stats"), sem("ln3_var"), sem("ln3_std"), sem("ln3_rstd"), sem("ln3_settled")
        W1 = w("W1")
        W2 = w("W2").rearrange("p (g n) -> p g n", g=G)
        out_view = out_dram.rearrange("(q p e) n d -> q e n p d", q=QUADS, e=2)

        with nc.Block() as block:
            @block.sync
            def _(sp):

                def quad(q):
                    sp.wait_ge(out_ready, q + 1)
                    settle(sp, sp_settled)
                    for e in range(2):
                        dst = out_view[bass.ds(q, 1), e, :, :, :].rearrange("o n p d -> n (o p) d")
                        sp.dma_start(dst, out_t[SLOT * e:SLOT * e + N, :].rearrange("r (p d) -> r p d", p=4)
                                     ).then_inc(stored, 16)

                quad(0)
                with sp.Fori(1, QUADS) as q:
                    quad(q)
                sp.wait_ge(stored, QUADS * 32)

            @block.gpsimd
            def _(pool):

                def quad(q):
                    wait_past(pool, x2_done, q)
                    settle(pool, pool_settled)
                    nc.gpsimd.tensor_copy(xs[:, :], x_all[:, bass.ds(q, 1), :].rearrange("p o n -> p (o n)")
                                          ).then_inc(xs_ready, 1)
                    for g in range(G):
                        pool.wait_ge(whole_ready, q * G + g + 1)
                        wait_past(pool, sine_ready, q * G + g - 1)
                        nc.gpsimd.tensor_tensor(frac[:, g % 2, :], turns[:, g % 2, :], whole[:, g % 2, :],
                                                ALU.subtract).then_inc(frac_ready, 1)

                quad(0)
                with pool.Fori(1, QUADS) as q:
                    quad(q)

            @block.scalar
            def _(act):
                def root(ln, k, q):
                    act.wait_ge(ln[1], q + 1)
                    nc.scalar.activation(std[k][:, :], mv[k][:, :, 1], ACT.Sqrt,
                                         bias=eps[:, 0:1]).then_inc(ln[2], 1)


                def quad(q):
                    root(ln2, 0, q)
                    act.wait_ge(x2T_ps, q + 1)
                    nc.scalar.copy(x2T[:, :], banks[0][:, :]).then_inc(x2T_sb, 1)

                    def turn(g):
                        act.wait_ge(h_ps, q * G + g + 1)
                        wait_past(act, frac_ready, q * G + g - 1)
                        nc.scalar.activation(turns[:, g % 2, :], banks[2 + g][:, :], ACT.Identity,
                                             bias=m["u_bias"][:, g:g + 1], scale=0.1 * INV2PI
                                             ).then_inc(turns_ready, 1)

                    turn(0)
                    for g in range(G):
                        if g + 1 < G:
                            turn(g + 1)
                        act.wait_ge(frac_ready, q * G + g + 1)
                        wait_past(act, z_ready, q * G + g - 1)
                        nc.scalar.activation(sine[:, g % 2, :], frac[:, g % 2, :], ACT.Sin,
                                             scale=TWO_PI_BELOW).then_inc(sine_ready, 1)
                        act.wait_ge(z_ready, q * G + g + 1)
                        nc.scalar.activation(hid[:, g, :], z[:, g % 2, :], ACT.Relu,
                                             bias=w("b1")[:, g:g + 1]).then_inc(hid_ready, 1)
                    root(ln3, 1, q)

                quad(0)
                with act.Fori(1, QUADS) as q:
                    quad(q)

            @block.tensor
            def _(pe):

                def quad(q):
                    pe.wait_ge(x2_done, q + 1)
                    for p in range(4):
                        last = nc.tensor.transpose(banks[0][:, p * P:(p + 1) * P], x2[:, p * D:(p + 1) * D], ident)
                    last.then_inc(x2T_ps, 1)
                    pe.wait_ge(x2T_sb, q + 1)
                    for g in range(G):
                        wait_past(pe, z_ready, q * G)
                        nc.tensor.matmul(banks[2 + g][:, :], W1[:, g * P:(g + 1) * P], x2T[:, :], start=True,
                                         stop=True).then_inc(h_ps, 1)
                    pe.wait_ge(hid_ready, (q + 1) * G)
                    wait_past(pe, y_done, q)
                    for p in range(4):
                        dst = banks[1][:, p * P:(p + 1) * P]
                        for g in range(G):
                            nc.tensor.matmul(dst, hid[:, g, p * P:(p + 1) * P], W2[:, g, :], start=(g == 0),
                                             stop=False)
                        last = nc.tensor.matmul(dst, ones[0:1, :], m["b2_row"], start=False, stop=True)
                    last.then_inc(f_ps, 1)

                quad(0)
                with pe.Fori(1, QUADS) as q:
                    quad(q)

            @block.vector
            def _(dve):

                def quad(q):
                    dve.wait_ge(xs_ready, q + 1)
                    layernorm_steps(nc, dve, xs, x2, stats[0], mv[0], std[0], rstd[0], ln2, q).then_inc(x2_done, 1)
                    for g in range(G):
                        dve.wait_ge(turns_ready, q * G + g + 1)
                        wait_past(dve, frac_ready, q * G + g - 1)
                        nc.vector.tensor_scalar(whole[:, g % 2, :], turns[:, g % 2, :], ROUND, -ROUND, ALU.add,
                                                ALU.add).then_inc(whole_ready, 1)
                        dve.wait_ge(sine_ready, q * G + g + 1)
                        wait_past(dve, hid_ready, q * G + g - 1)
                        nc.vector.scalar_tensor_tensor(z[:, g % 2, :], sine[:, g % 2, :], m["s_coef"][:, g:g + 1],
                                                       banks[2 + g][:, :], ALU.mult, ALU.add).then_inc(z_ready, 1)
                    dve.wait_ge(f_ps, q + 1)
                    nc.vector.tensor_tensor(y[:, :], banks[1][:, :], x2[:, :], ALU.add).then_inc(y_done, 1)
                    dve.wait_ge(y_done, q + 1)
                    wait_past(dve, stored, q * 32)
                    layernorm_steps(nc, dve, y, out_t, stats[1], mv[1], std[1], rstd[1], ln3,
                                    q).then_inc(out_ready, 1)

                quad(0)
                with dve.Fori(1, QUADS) as q:
                    quad(q)
def pack_inputs(i):
    t = {name: np.zeros((P, width), np.float32) for name, (_, width) in PACK.items()}
    f = {k: np.asarray(v) for k, v in i.items()}
    part = np.arange(P)
    t["ident"][part, part] = 1
    wqkv = f["L0_attn_w_qkv"]
    t["wqT"][:], t["wkT"][:], t["wv"][:] = wqkv[:, 0:D].T, wqkv[:, D:2 * D].T, wqkv[:, 2 * D:]
    for h in range(H):
        t["proj"][h * HD:(h + 1) * HD, h * FEAT:(h + 1) * FEAT] = f["L0_attn_proj_matrix"][h]
    t["w_out"][:] = f["L0_attn_w_out"]
    for name in ("Wq", "Wk", "Wv", "Wo"):
        t[name + "T"][:] = f["L0_xattn_" + name].T
    for h in range(H):
        j, s = divmod(h, 4)
        at = 32 * j + (8 + 8 * s if s < 3 else 0)
        t["WoSlots"][at:at + HD, s * P:(s + 1) * P] = f["L0_xattn_Wo"].T[h * HD:(h + 1) * HD]
    t["selA"][32 * (part // 32), part] = 1
    t["selB"][32 * (part // 32) + 8, part] = 1
    for a in range(8):
        for h in range(4):
            t["maskKV"][32 * h:32 * h + 32, a * KVW + 8 * h:a * KVW + 8 * h + 8] = 1
            t["maskKV"][32 * h:32 * h + 32, a * KVW + 32 + h] = 1
    for h in range(4):
        t["maskQ"][part % 32 // HD == h, h] = 1
    for h in range(H):
        t["maskM"][part // HD == h, h] = 1
    t["W1"][:] = f["L0_ffn_W1"]
    t["W2"][:] = f["L0_ffn_W2"].reshape(4, P, D).transpose(1, 0, 2).reshape(P, 4 * D)
    for name, key in (("bq", "L0_xattn_bq"), ("bk", "L0_xattn_bk"), ("bv", "L0_xattn_bv")):
        t[name][:, 0] = f[key]
    for name, key in (("b1", "L0_ffn_b1"), ("theta", "L0_ffn_quantum_phases"),
                      ("wr", "L0_ffn_quantum_weights_real"), ("wi", "L0_ffn_quantum_weights_imag")):
        t[name][:] = f[key].reshape(4, P).T
    for n, key in enumerate(("L0_attn_b_out", "L0_xattn_bo", "L0_ffn_b2")):
        t["rows"][0, n * P:(n + 1) * P] = f[key]
    return np.ascontiguousarray(np.concatenate([t[name] for name in PACK], axis=1))


def kernel(**inputs):
    import concourse.bacc as bacc
    from concourse.bass_utils import run_bass_kernel_spmd

    nc = bacc.Bacc("TRN2", target_bir_lowering=False, num_devices=1)
    arrays = {"ctx_in": np.ascontiguousarray(inputs["ctx_1024"]), "x_in": np.ascontiguousarray(inputs["x"]),
              "pack_in": pack_inputs(inputs)}
    drams = [nc.dram_tensor(name, a.shape, F32, kind="ExternalInput").ap() for name, a in arrays.items()]
    out = nc.dram_tensor("out", (B, N, D), F32, kind="ExternalOutput").ap()
    build(nc, *drams, out)
    return run_bass_kernel_spmd(nc, [arrays], core_ids=[0]).results[0]["out"]
```

```python
from contextlib import ExitStack

import numpy as np

import concourse.bass as bass
from concourse import mybir

F32 = mybir.dt.float32
F16 = mybir.dt.float16
ALU = mybir.AluOpType
ACT = mybir.ActivationFunctionType
AX = mybir.AxisListType

P = 128
B, N, D = 32, 56, 128
S = 1500
H, HD = 16, 8
FEAT = 32
FF = 512
SLOT = 64
QUADS = B // 8
QT = 8 * SLOT
G = 4
GC = 4 * N
HQ = H * N
KP = 125
KT = S // KP
KC = 3
CH = S // KC
MB = HQ // P
NM = MB * KC
ROWS = 97
SHIFT = 64.0
PBUF = 4
RING = 3
KVW = 33
SCALE = float(HD) ** -0.5
EPS = 1e-5
ROUND = 1.5 * 2.0 ** 23
INV2PI = float(1.0 / (2.0 * np.pi))
TWO_PI_BELOW = 6.283185
C1 = 6.28125
C2 = 0.0019350051879882812
C3 = float(2.0 * np.pi - C1 - C2)

PACK = {}
_at = 0
for _name, _w in (("ident", P), ("wqT", P), ("wkT", P), ("wv", P), ("proj", H * FEAT), ("w_out", P),
                  ("WqT", P), ("bq", 1), ("maskKV", 32), ("rows", 3 * P),
                  ("WkT", P), ("WvT", P), ("WoT", P), ("WoSlots", 4 * P), ("selA", P),
                  ("selB", P), ("maskQ", 4), ("maskM", H), ("W1", FF), ("W2", FF),
                  ("bk", 1), ("bv", 1), ("b1", 4), ("theta", 4), ("wr", 4), ("wi", 4)):
    PACK[_name] = (_at, _w)
    _at += _w
PACKW = _at
PACK_FIRST = PACK["WkT"][0]


def wait_past(engine, semaphore, count):
    if not isinstance(count, int) or count > 0:
        engine.wait_ge(semaphore, count)


def settle(engine, counter):
    engine.nop().then_inc(counter, 1)


EPILOGUE = (("R", 0), ("R", 1), ("Y", 0))
TAIL = [("K", c) for c in range(KC)]


def unit_plan(u):
    steps = [[] for _ in range(KT)]
    m = 0
    for t, count in enumerate((2, 1, 2, 2, 2, 3, 3, 3, 3) if u == 0 else (3, 2, 2, 3, 2, 2, 3, 2, 2)):
        for _ in range(count):
            steps[t].append(("M", m))
            m += 1
    if u == 0:
        steps[1] = [("R", 0), ("R", 1)] + steps[1]
        steps[3] = [("Y", 0)] + steps[3]
    for c, t in enumerate((4, 6, 8) if u == 0 else (3, 5, 7)):
        steps[t].append(("V", c))
    steps[9] += [("T", 0), ("T", 1)]
    steps[10] += [("T", 2)]
    return steps


def ring_slots(u):
    order = [unit for step in unit_plan(u) for unit in step] + TAIL
    assert len(order) % RING == 0
    return {unit: k % RING for k, unit in enumerate(order)}


def build(nc, ctx_dram, x_dram, pack_dram, out_dram):
    with ExitStack() as stack:
        pack = stack.enter_context(nc.sbuf_tensor("pack", [P, PACKW], F32))

        def w(name):
            at, width = PACK[name]
            return pack[:, at:at + width]

        row_at = PACK["rows"][0]
        shared = {
            "pack": pack, "w": w, "ident": w("ident"), "wslots": w("WoSlots").rearrange("p (s n) -> p s n", s=4),
            "b_out_row": pack[0:1, row_at:row_at + P],
            "bo_row": pack[0:1, row_at + P:row_at + 2 * P],
            "b2_row": pack[0:1, row_at + 2 * P:row_at + 3 * P],
        }
        for name, shape in (("eps", [P, 1]), ("b2_all", [P, P]), ("x_all", [P, QUADS, 4 * D]),
                            ("u_bias", [P, 4]), ("s_coef", [P, 4])):
            shared[name] = stack.enter_context(nc.sbuf_tensor(name, shape, F32))
        psum = stack.enter_context(nc.psum_tensor("psum", [P, 8, 512], F32))
        shared["psum"], shared["banks"] = psum, [psum[:, i, :] for i in range(8)]
        attention_block(nc, ctx_dram, x_dram, pack_dram, shared)
        ffn_block(nc, out_dram, shared)


def ln_stats(dve, src, stats, mv, sems, q):
    stats_done, var_ready, settled = sems
    for p in range(4):
        last = dve.bn_stats(stats[:, p, :], src[:, p * D:(p + 1) * D])
    last.then_inc(stats_done, 1)
    dve.wait_ge(stats_done, q + 1)
    settle(dve, settled)
    for p in range(4):
        last = dve.bn_aggr(mv[:, p, :], stats[:, p, :])
    last.then_inc(var_ready, 1)


def ln_apply(dve, src, dst, mv, std, rstd, std_ready, rstd_ready, q):
    dve.wait_ge(std_ready, q + 1)
    dve.reciprocal(rstd[:, :], std[:, :]).then_inc(rstd_ready, 1)
    dve.wait_ge(rstd_ready, q + 1)
    for p in range(4):
        last = dve.tensor_scalar(dst[:, p * D:(p + 1) * D], src[:, p * D:(p + 1) * D],
                                 mv[:, p, 0:1], rstd[:, p:p + 1], ALU.subtract, ALU.mult)
    return last


def attention_block(nc, ctx_dram, x_dram, pack_dram, m):
    pack, w, ident, eps, b2_all, wslots = (m[k] for k in ("pack", "w", "ident", "eps", "b2_all", "wslots"))
    x_all, psum, banks, u_bias, s_coef = (m[k] for k in ("x_all", "psum", "banks", "u_bias", "s_coef"))
    x_pairs = x_all[:, :, :].rearrange("p q (a d) -> p (q a) d", a=4)
    TPB = 8
    slots = [ring_slots(0), ring_slots(1)]
    plans = [unit_plan(0), unit_plan(1)]

    with ExitStack() as stack:
        def sb(name, shape, dt=F32):
            return stack.enter_context(nc.sbuf_tensor(name, shape, dt))

        def sem(name):
            return stack.enter_context(nc.semaphore(name))

        wqp, wkp = sb("wqp", [P, H * FEAT]), sb("wkp", [P, H * FEAT])
        WkH, WkL = sb("WkH", [P, P], F16), sb("WkL", [P, P], F16)
        WvH, WvL = sb("WvH", [P, P], F16), sb("WvL", [P, P], F16)
        ones = sb("ones", [P, P])
        eps_z = sb("eps_z", [P, 1])
        b_all = sb("b_all", [P, P])
        xq = sb("xq", [P, 4 * D])
        xres = sb("xres", [P, 4 * D])
        xT = sb("xT", [P, QT])
        e_buf = sb("e_buf", [P, 4, 512])
        kf = sb("kf", [P, 4, H * FEAT])
        qf = sb("qf", [P, G, QT])
        v_s = sb("v_s", [P, 4 * G, KVW])
        kvn = sb("kvn", [P, 2, 2, 8, 32])
        kvd = sb("kvd", [P, 2, 2, 8, 32])
        den = sb("den", [P, QT])
        rden = sb("rden", [P, QT])
        aT = sb("aT", [P, QT])
        xr = sb("xr", [P, 4 * D])
        x1 = sb("x1", [P, 4 * D])
        x1T = sb("x1T", [P, QT])
        qh = sb("qh", [P, B * SLOT], F16)
        ql = sb("ql", [P, B * SLOT], F16)
        q_stack = sb("q_stack", [96, G, B * SLOT], F16)
        stats, mv = sb("stats", [P, 4, 6]), sb("mv", [P, 4, 2])
        std, rstd = sb("std", [P, 4]), sb("rstd", [P, 4])
        ang = sb("ang", [P, 8, 4])
        theta_r = sb("theta_r", [P, 4])

        pack_first, pack_rest, x_zeroed = sem("pack_first"), sem("pack_rest"), sem("x_zeroed")
        x_first, x_rest, consts = sem("x_first"), sem("x_rest"), sem("consts")
        fold_ps, fold_sb, row_ps, row_done = sem("fold_ps"), sem("fold_sb"), sem("row_ps"), sem("row_done")
        split_hi, split_done = sem("split_hi"), sem("split_done")
        c_step, turns_in, sin_done = sem("c_step"), sem("turns_in"), sem("sin_done")
        xq_ready, xres_ready, xT_ps, xT_sb = sem("xq_ready"), sem("xres_ready"), sem("xT_ps"), sem("xT_sb")
        feat_ps, feat_exp, feat_min, feat_done = sem("feat_ps"), sem("feat_exp"), sem("feat_min"), sem("feat_done")
        v_ps, v_sb, kv_ps, kv_sb = sem("v_ps"), sem("v_sb"), sem("kv_ps"), sem("kv_sb")
        at_ps, den_done, rden_done, aT_done = sem("at_ps"), sem("den_done"), sem("rden_done"), sem("aT_done")
        yo_ps, xr_done = sem("yo_ps"), sem("xr_done")
        ln1_stats, ln1_var, ln1_std, ln1_rstd = sem("ln1_stats"), sem("ln1_var"), sem("ln1_std"), sem("ln1_rstd")
        x1_done, x1_kept = sem("x1_done"), sem("x1_kept")
        x1T_ps, x1T_sb, q_ps, qh_done, ql_done = (sem("x1T_ps"), sem("x1T_sb"), sem("q_ps"), sem("qh_done"),
                                                  sem("ql_done"))
        q_stacked = sem("q_stacked")
        sp_settled, pool_settled, dve_settled = sem("sp_settled"), sem("pool_settled"), sem("dve_settled")
        mask_kv = w("maskKV").rearrange("p (e a c) -> p e a c", e=1, a=1).to_broadcast([P, 2, 8, 32])
        x_view = x_dram.rearrange("(a e) n d -> e n a d", e=2)
        YO = banks[7]

        c_in = sb("c_in", [P, 2, KT * D])
        c_hl = sb("c_hl", [P, 2 * KT, D], F16)
        cT = sb("cT", [P, 2 * KT, P], F16)
        kh, kl = sb("kh", [P, S], F16), sb("kl", [P, S], F16)
        k_stack = [sb(f"k_stack{i}", [P, G, S + 4], F16) for i in range(2)]
        q_diag = [sb(f"q_diag{i}", [P, HQ], F16) for i in range(2)]
        q_max = [sb(f"q_max{i}", [P, HQ], F16) for i in range(2)]
        v_ext = [sb(f"v_ext{i}", [P, KT, G, 48]) for i in range(2)]
        probs = sb("probs", [P, PBUF, HQ])
        mx = sb("mx", [P, NM])
        mrow = sb("mrow", [P, MB])
        m16, mT = sb("m16", [P, 32], F16), sb("mT", [P, 32], F16)
        ident16 = sb("ident16", [P, P], F16)
        o_sb = sb("o_sb", [P, 2, GC])
        r_sb = sb("r_sb", [P, 2, GC])
        o_n = sb("o_n", [P, 4, 2, SLOT])

        c_loaded, c_hi, c_split = [sem("c_loaded0"), sem("c_loaded1")], sem("c_hi"), sem("c_split")
        ready = {k: sem(f"unit_{k}") for k in "TKVMRY"}
        cT_done, kh_done, kl_done, v_done, mx_done = (sem("cT_done"), sem("kh_done"), sem("kl_done"),
                                                      sem("v_done"), sem("mx_done"))
        m_fold, m_cast, m_ready, m_placed = sem("m_fold"), sem("m_cast"), sem("m_ready"), sem("m_placed")
        qd_ready, qm_ready, k_stacked = sem("qd_ready"), sem("qm_ready"), sem("k_stacked")
        s_ready, p_ready, pv_done = sem("s_ready"), sem("p_ready"), sem("pv_done")
        o_copied, r_inv, o_ready, y_added = sem("o_copied"), sem("r_inv"), sem("o_ready"), sem("y_added")
        init, o_zeroed = sem("init"), sem("o_zeroed")
        INIT = 3 + 7

        scores = [psum[:, 0:2, :], psum[:, 2:4, :]]
        ring = banks[4:7]
        O = banks[7]
        PER = {"T": 3, "K": 3, "V": 3, "M": NM, "R": 2, "Y": 1}
        DONE = {"T": cT_done, "K": kl_done, "V": v_done, "M": mx_done, "R": r_inv, "Y": y_added}

        with nc.Block() as block:
            @block.sync
            def _(sp):
                sp.dma_start(pack[:, 0:PACK_FIRST], pack_dram[:, 0:PACK_FIRST]).then_inc(pack_first, 16)
                sp.wait_ge(x_zeroed, 1)
                for e in range(2):
                    sp.dma_start(x_pairs[SLOT * e:SLOT * e + N, 0:4, :], x_view[e, :, 0:4, :]
                                 ).then_inc(x_first, 16)
                sp.dma_start(pack[:, PACK_FIRST:], pack_dram[:, PACK_FIRST:]).then_inc(pack_rest, 16)
                for e in range(2):
                    sp.dma_start(x_pairs[SLOT * e:SLOT * e + N, 4:, :], x_view[e, :, 4:, :]
                                 ).then_inc(x_rest, 16)

                def load(n, buf):
                    src = ctx_dram[bass.ds(n, 1), :, :].rearrange("o (p t) d -> p (o t d)", t=KT)
                    sp.dma_start(c_in[0:KP, buf, :], src).then_inc(c_loaded[buf], 16)

                load(0, 0)
                load(1, 1)

                def stack_q(q):
                    sp.wait_ge(ql_done, q + 1)
                    settle(sp, sp_settled)
                    wait_past(sp, q_stacked, q * 192)
                    if not isinstance(q, int):
                        settle(sp, sp_settled)
                    for c, part in enumerate((qh, ql, qh)):
                        for g in range(G):
                            sp.dma_start(q_stack[32 * c:32 * c + 32, g, bass.ds(q * QT, QT)],
                                         part[32 * g:32 * g + 32, bass.ds(q * QT, QT)]).then_inc(q_stacked, 16)

                stack_q(0)
                with sp.Fori(1, QUADS) as q:
                    stack_q(q)

                def stack_k(n, u):
                    sp.wait_ge(kl_done, (n + 1) * KC)
                    settle(sp, sp_settled)
                    for c, part in enumerate((kh, kh, kl)):
                        for g in range(G):
                            sp.dma_start(k_stack[u][32 * c:32 * c + 32, g, 0:S],
                                         part[32 * g:32 * g + 32, :]).then_inc(k_stacked, 16)

                def place_m(n, u):
                    sp.wait_ge(m_ready, n + 1)
                    settle(sp, sp_settled)
                    row = q_diag[u][96:97, :].rearrange("o (r q i) -> o r q i", q=4, i=32)
                    for quarter in range(4):
                        sp.dma_start(row[:, :, quarter, :],
                                     mT[32 * quarter:32 * quarter + MB, :]).then_inc(m_placed, 16)

                sp.wait_ge(init, INIT)
                stack_k(0, 0)
                load(2, 0)
                sp.wait_ge(c_split, 2)
                load(3, 1)
                place_m(0, 0)

                def body(b, u, stage2, load4):
                    if load4:
                        sp.wait_ge(c_split, b + 3)
                        settle(sp, sp_settled)
                        load(b + 4, u)
                    if stage2:
                        wait_past(sp, s_ready, b * KT)
                        settle(sp, sp_settled)
                        stack_k(b + 1, 1 - u)
                        place_m(b + 1, 1 - u)

                for b in range(2):
                    body(b, b, True, True)
                with sp.Fori(1, (B - 4) // 2) as i:
                    for u in range(2):
                        body(i * 2 + u, u, True, True)
                for b in range(B - 4, B):
                    body(b, b % 2, b + 1 < B, b + 4 < B)

            @block.gpsimd
            def _(pool):
                pool.memset(x_all[:, :, :], 0.0).then_inc(x_zeroed, 1)
                for t, value in ((ones, 1.0), (v_s, 1.0), (eps, EPS), (eps_z, 1e-8)):
                    pool.memset(t[:], value).then_inc(consts, 1)
                for t in v_ext:
                    pool.memset(t[:, :, :, :], 1.0).then_inc(init, 1)
                pool.memset(m16[:, :], 0.0).then_inc(init, 1)

                def quad_in(q, first):
                    if first:
                        pool.wait_ge(x_first, 32)
                    else:
                        pool.wait_ge(x_rest, 32)
                        pool.wait_ge(xT_ps, q)
                        settle(pool, pool_settled)
                    x_of_quad = x_all[:, bass.ds(q, 1), :].rearrange("p o n -> p (o n)")
                    nc.gpsimd.tensor_copy(xq[:, :], x_of_quad).then_inc(xq_ready, 1)
                    if first:
                        pool.wait_ge(row_done, 2)
                    else:
                        pool.wait_ge(xr_done, q)
                        settle(pool, pool_settled)
                    nc.gpsimd.tensor_tensor(
                        xres[:, :].rearrange("p (a d) -> p a d", a=4), x_of_quad.rearrange("p (a d) -> p a d", a=4),
                        b_all[:, :].rearrange("p (o d) -> p o d", o=1).to_broadcast([P, 4, D]),
                        ALU.add).then_inc(xres_ready, 1)

                def keep_x1(q):
                    pool.wait_ge(x1_done, q + 1)
                    pool.wait_ge(xres_ready, q + 1)
                    settle(pool, pool_settled)
                    nc.gpsimd.tensor_copy(x_all[:, bass.ds(q, 1), :].rearrange("p o n -> p (o n)"),
                                          x1[:, :]).then_inc(x1_kept, 1)

                def split(n, buf, half):
                    pool.wait_ge(c_loaded[buf], half * 16 + 16)
                    settle(pool, pool_settled)
                    src = c_in[0:KP, buf, :].rearrange("p (t d) -> p t d", t=KT)
                    nc.gpsimd.tensor_copy(c_hl[0:KP, 0:KT, :], src).then_inc(c_hi, 1)
                    pool.wait_ge(c_hi, n + 1)
                    nc.gpsimd.tensor_tensor(c_hl[0:KP, KT:2 * KT, :], src, c_hl[0:KP, 0:KT, :],
                                            ALU.subtract).then_inc(c_split, 1)

                def diag_q(n, u):
                    q = q_stack[0:96, :, bass.ds(n * SLOT, N)].rearrange("p g (o n) -> p g o n", o=1)
                    nc.gpsimd.tensor_tensor(
                        q_diag[u][0:96, :].rearrange("p (g h n) -> p g h n", g=G, h=4),
                        q.to_broadcast([96, G, 4, N]),
                        w("maskQ")[0:96, :].rearrange("p (o h e) -> p o h e", o=1, e=1).to_broadcast([96, G, 4, N]),
                        ALU.mult).then_inc(qd_ready, 1)

                def max_q(n, u):
                    q = qh[:, bass.ds(n * SLOT, N)].rearrange("p (o n) -> p o n", o=1)
                    nc.gpsimd.tensor_tensor(
                        q_max[u][:, :].rearrange("p (h n) -> p h n", h=H), q.to_broadcast([P, H, N]),
                        w("maskM").rearrange("p (h o) -> p h o", o=1).to_broadcast([P, H, N]),
                        ALU.mult).then_inc(qm_ready, 1)

                quad_in(0, True)
                with pool.Fori(1, QUADS) as q:
                    quad_in(q, False)
                    keep_x1(q - 1)
                pool.wait_ge(init, INIT)
                split(0, 0, 0)
                pool.wait_ge(q_stacked, 192)
                pool.wait_ge(pack_rest, 16)
                max_q(0, 0)
                diag_q(0, 0)
                max_q(1, 1)
                keep_x1(QUADS - 1)
                pool.wait_ge(ready["T"], 3)
                split(1, 1, 0)
                pool.wait_ge(ready["T"], 6)
                split(2, 0, 1)
                pool.wait_ge(q_stacked, 192 * QUADS)

                def body(b, pair, u, s1, s2, s3):
                    if s2:
                        wait_past(pool, s_ready, b * KT)
                        settle(pool, pool_settled)
                        diag_q(b + 1, 1 - u)
                    if s1:
                        pool.wait_ge(ready["M"], (b + 1) * NM)
                        settle(pool, pool_settled)
                        max_q(b + 2, u)
                    if s3:
                        pool.wait_ge(ready["T"], b * 3 + 9)
                        split(b + 3, 1 - u, pair + 1 + u)

                for b in range(2):
                    body(b, 0, b, True, True, True)
                with pool.Fori(1, (B - 4) // 2) as i:
                    for u in range(2):
                        body(i * 2 + u, i, u, True, True, True)
                for b in range(B - 4, B):
                    body(b, b // 2, b % 2, b + 2 < B, b + 1 < B, b + 3 < B)

            @block.scalar
            def _(act):
                for i, dst in enumerate((wqp, wkp)):
                    act.wait_ge(fold_ps, i + 1)
                    nc.scalar.copy(dst[:, :], banks[2 + i]).then_inc(fold_sb, 1)
                act.wait_ge(consts, 4)

                def front(q, back):
                    act.wait_ge(xT_ps, q + 1)
                    nc.scalar.copy(xT[:, :], banks[0]).then_inc(xT_sb, 1)
                    act.wait_ge(v_ps, q + 1)
                    nc.scalar.copy(v_s[:, :, 0:32], banks[1].rearrange("p (a c) -> p a c", c=32)).then_inc(v_sb, 1)
                    for u in range(8):
                        if u == 4 and back:
                            root(q - 1)
                        act.wait_ge(feat_ps, q * 8 + u + 1)
                        wait_past(act, feat_done, q * 8 + u - 3)
                        nc.scalar.activation(e_buf[:, u % 4, :], banks[2 + u % 4], ACT.Exp).then_inc(feat_exp, 1)
                    if back:
                        x1_T(q - 1)
                        q_hi(q - 1)
                    act.wait_ge(at_ps, q + 1)
                    nc.scalar.activation(den[:, :], banks[3], ACT.Identity, bias=eps_z[:, 0:1]).then_inc(den_done, 1)

                def root(q):
                    act.wait_ge(ln1_var, q + 1)
                    nc.scalar.activation(std[:, :], mv[:, :, 1], ACT.Sqrt, bias=eps[:, 0:1]).then_inc(ln1_std, 1)

                def x1_T(q):
                    act.wait_ge(x1T_ps, q + 1)
                    nc.scalar.copy(x1T[:, :], banks[0]).then_inc(x1T_sb, 1)

                def q_hi(q):
                    act.wait_ge(q_ps, q + 1)
                    nc.scalar.activation(qh[:, bass.ds(q * QT, QT)], banks[1], ACT.Identity,
                                         bias=w("bq")).then_inc(qh_done, 1)

                def exp(b, t):
                    act.wait_ge(s_ready, b * KT + t + 1)
                    wait_past(act, pv_done, b * KT + t - PBUF + 1)
                    nc.scalar.activation(probs[0:KP, t % PBUF, :].rearrange("p (a c) -> p a c", a=2),
                                         scores[t % 2][0:KP, :, 0:2 * GC], ACT.Exp, scale=SCALE).then_inc(p_ready, 1)

                def v_copy(n, i, u, bank):
                    act.wait_ge(ready["V"], n * 3 + i + 1)
                    nc.scalar.copy(v_ext[u][0:KP, 4 * i:4 * i + 4, :, 8:40],
                                   bank[0:KP, :].rearrange("p (t j c) -> p t j c", t=4, j=G)).then_inc(v_done, 1)

                def k_hi(n, i):
                    act.wait_ge(ready["K"], n * 3 + i + 1)
                    if i == 0:
                        wait_past(act, ready["M"], n * NM)
                        wait_past(act, k_stacked, n * 192)
                    nc.scalar.activation(kh[:, i * CH:(i + 1) * CH], ring[i][:, 0:CH], ACT.Identity,
                                         bias=w("bk")).then_inc(kh_done, 1)

                front(0, False)
                with act.Fori(1, QUADS) as q:
                    front(q, True)
                act.wait_ge(init, INIT)
                root(QUADS - 1)
                x1_T(QUADS - 1)
                for i in range(3):
                    k_hi(0, i)
                q_hi(QUADS - 1)
                act.wait_ge(turns_in, 1)
                nc.scalar.activation(ang[:, 3:5, :], ang[:, 1:3, :], ACT.Sin, scale=TWO_PI_BELOW).then_inc(sin_done, 1)
                for i in range(3):
                    v_copy(0, i, 0, ring[i])
                for i in range(3):
                    k_hi(1, i)

                def body(b, u, s1, s2):
                    for t in range(KT):
                        exp(b, t)
                        for kind, i in plans[u][t]:
                            if kind == "V" and s2:
                                v_copy(b + 1, i, 1 - u, ring[slots[u][kind, i]])
                    if s1:
                        for i in range(3):
                            k_hi(b + 2, i)

                for b in range(2):
                    body(b, b % 2, True, True)
                with act.Fori(1, B // 2 - 1) as i:
                    for u in range(2):
                        body(i * 2 + u, u, True, True)
                for b in range(B - 2, B):
                    body(b, b % 2, b + 2 < B, b + 1 < B)

            @block.tensor
            def _(pe):
                pe.wait_ge(pack_first, 16)
                for i, name in enumerate(("wqT", "wkT")):
                    nc.tensor.matmul(banks[2 + i], w(name), w("proj"), start=True, stop=True).then_inc(fold_ps, 1)
                pe.wait_ge(consts, 4)
                nc.tensor.matmul(banks[4][:, 0:P], ones[0:1, :], m["b_out_row"], start=True, stop=True)
                nc.tensor.matmul(banks[4][:, P:2 * P], ones[0:1, :], m["b2_row"], start=True,
                                 stop=True).then_inc(row_ps, 1)
                pe.wait_ge(fold_sb, 2)
                pe.wait_ge(row_done, 2)

                def x_T(q):
                    pe.wait_ge(xq_ready, q + 1)
                    for p in range(4):
                        last = nc.tensor.transpose(banks[0][:, p * P:(p + 1) * P], xq[:, p * D:(p + 1) * D], ident)
                    last.then_inc(xT_ps, 1)

                def values(q):
                    pe.wait_ge(xT_sb, q + 1)
                    wait_past(pe, aT_done, q)
                    for p in range(4):
                        last = nc.tensor.matmul(banks[1][:, p * P:(p + 1) * P], xT[:, p * P:(p + 1) * P], w("wv"),
                                                start=True, stop=True)
                    last.then_inc(v_ps, 1)

                def features(q, u):
                    wait_past(pe, feat_done, q * 8 + u - 3)
                    if u == 1:
                        wait_past(pe, den_done, q)
                    if u < 4:
                        mm = nc.tensor.matmul(banks[2 + u], xT[:, u * P:(u + 1) * P], wkp[:, :], start=True, stop=True)
                    else:
                        mm = nc.tensor.matmul(banks[u - 2], wqp[:, (u - 4) * P:(u - 3) * P], xT[:, :], start=True,
                                              stop=True)
                    mm.then_inc(feat_ps, 1)

                def key_values(q):
                    pe.wait_ge(v_sb, q + 1)
                    wait_past(pe, xr_done, q)
                    for i in range(2):
                        pe.wait_ge(feat_done, q * 8 + 2 * i + 2)
                        wait_past(pe, kv_sb, q * 2 + i)
                        for p in (2 * i, 2 * i + 1):
                            for e in range(2):
                                rows = slice(SLOT * e, SLOT * e + N)
                                for g in range(G):
                                    at = (4 * (p % 2) + g) * KVW
                                    last = nc.tensor.matmul(banks[6 + e][:, at:at + KVW], kf[rows, p, g * P:(g + 1) * P],
                                                            v_s[rows, p * G + g, :], start=True, stop=True)
                        last.then_inc(kv_ps, 1)

                def attend(q):
                    pe.wait_ge(feat_done, q * 8 + 8)
                    pe.wait_ge(kv_sb, q * 2 + 2)
                    for p in range(4):
                        for e in range(2):
                            tok = slice(p * P + SLOT * e, p * P + SLOT * e + SLOT)
                            for bank, sums in ((banks[2], kvn), (banks[3], kvd)):
                                for g in range(G):
                                    last = nc.tensor.matmul(bank[32 * g:32 * g + 32, tok],
                                                            sums[:, p // 2, e, 4 * (p % 2) + g, :], qf[:, g, tok],
                                                            start=True, stop=True)
                    last.then_inc(at_ps, 1)

                def out_projection(q):
                    pe.wait_ge(aT_done, q + 1)
                    wait_past(pe, kv_sb, q * 2 + 2)
                    for p in range(4):
                        last = nc.tensor.matmul(YO[:, p * P:(p + 1) * P], aT[:, p * P:(p + 1) * P], w("w_out"),
                                                start=True, stop=True)
                    last.then_inc(yo_ps, 1)

                def x1_T(q):
                    pe.wait_ge(x1_done, q + 1)
                    for p in range(4):
                        last = nc.tensor.transpose(banks[0][:, p * P:(p + 1) * P], x1[:, p * D:(p + 1) * D], ident)
                    last.then_inc(x1T_ps, 1)

                def queries(q):
                    pe.wait_ge(x1T_sb, q + 1)
                    nc.tensor.matmul(banks[1], w("WqT"), x1T[:, :], start=True, stop=True).then_inc(q_ps, 1)

                def front(q, back):
                    x_T(q)
                    values(q)
                    features(q, 0)
                    features(q, 1)
                    if back:
                        out_projection(q - 1)
                    for u in range(2, 8):
                        features(q, u)
                    if back:
                        x1_T(q - 1)
                    key_values(q)
                    if back:
                        queries(q - 1)
                    attend(q)

                front(0, False)
                with pe.Fori(1, QUADS) as q:
                    front(q, True)

                def unit(kind, i, n, u, slot, before):
                    if before is not None:
                        held, j, k = before
                        pe.wait_ge(DONE[held], k * PER[held] + j + 1)
                    bank = ring[slot]
                    if kind == "T":
                        if i == 0:
                            pe.wait_ge(c_split, n + 1)
                        out = bank.bitcast(F16).rearrange("p (t k) -> p t k", t=TPB)
                        for j in range(TPB):
                            last = nc.tensor.transpose(out[:, j, :], c_hl[:, i * TPB + j, :], ident16[:, :])
                    elif kind == "K":
                        if i == 0:
                            pe.wait_ge(cT_done, n * 3 + 3)
                        for k, (wt, part) in enumerate(((WkH, 0), (WkH, KT), (WkL, 0))):
                            last = nc.tensor.matmul(bank[:, 0:CH], wt[:, :],
                                                    cT[:, part + 4 * i:part + 4 * i + 4, 0:KP],
                                                    start=(k == 0), stop=(k == 2))
                    elif kind == "V":
                        for j in range(4):
                            for k, (part, wt) in enumerate(((0, WvH), (KT, WvH), (0, WvL))):
                                last = nc.tensor.matmul(bank[:, j * P:(j + 1) * P], cT[:, part + 4 * i + j, :],
                                                        wt[:, :], start=(k == 0), stop=(k == 2))
                    elif kind == "M":
                        r, c = divmod(i, KC)
                        if i == 0:
                            pe.wait_ge(kh_done, n * KC + KC)
                            pe.wait_ge(qm_ready, n + 1)
                        last = nc.tensor.matmul(bank[:, 0:CH], q_max[u][:, r * P:(r + 1) * P],
                                                kh[:, c * CH:(c + 1) * CH], start=True, stop=True)
                    elif kind == "R":
                        if i == 0:
                            pe.wait_ge(o_copied, n * 2 + 2)
                            last = nc.tensor.matmul(bank[:, 0:6 * N], w("selA"), o_sb[:, :, 0:3 * N], start=True,
                                                    stop=True)
                        else:
                            last = nc.tensor.matmul(bank[:, 0:2 * N], w("selB"), o_sb[:, :, 3 * N:GC], start=True,
                                                    stop=True)
                    else:
                        pe.wait_ge(o_ready, n + 1)
                        for s in range(4):
                            last = nc.tensor.matmul(bank[:, 0:D], o_n[:, s, :, :].rearrange("p e n -> p (e n)"),
                                                    wslots[:, s, :], start=(s == 0), stop=(s == 3))
                    last.then_inc(ready[kind], 1)

                def score(b, t, u):
                    if t == 0:
                        pe.wait_ge(k_stacked, (b + 1) * 16 * 12)
                        pe.wait_ge(qd_ready, b + 1)
                        pe.wait_ge(m_placed, (b + 1) * 64)
                    wait_past(pe, p_ready, b * KT + t - 1)
                    for g in range(G):
                        last = nc.tensor.matmul(scores[t % 2][:, g // 2, (g % 2) * GC:(g % 2 + 1) * GC],
                                                k_stack[u][0:ROWS, g, t * KP:t * KP + P],
                                                q_diag[u][0:ROWS, g * GC:(g + 1) * GC], start=True, stop=True)
                    last.then_inc(s_ready, 1)

                def pv(b, t, u):
                    if t == 0:
                        pe.wait_ge(v_done, b * 3 + 3)
                        wait_past(pe, o_copied, b)
                    pe.wait_ge(p_ready, b * KT + t + 1)
                    for j in range(G):
                        at = j * GC
                        nc.tensor.matmul(O[32 * j:32 * j + 32, 0:3 * N], v_ext[u][0:KP, t, j, 0:32],
                                         probs[0:KP, t % PBUF, at:at + 3 * N], start=(t == 0), stop=(t == KT - 1),
                                         skip_group_check=True)
                    for j in range(G):
                        at = j * GC
                        last = nc.tensor.matmul(O[32 * j:32 * j + 16, 3 * N:GC], v_ext[u][0:KP, t, j, 32:48],
                                                probs[0:KP, t % PBUF, at + 3 * N:at + GC], start=False,
                                                stop=(t == KT - 1), skip_group_check=True)
                    last.then_inc(pv_done, 1)

                def body(b, pair, u, s1, s2, epilogue):
                    held = [("K", c, b + 1) for c in range(KC)]

                    def go(kind, i):
                        n = {"T": b + 2, "K": b + 2, "R": pair - 1, "Y": pair - 1}.get(kind, b + 1)
                        wanted = {"T": s1, "K": s1, "R": epilogue, "Y": epilogue}.get(kind, s2)
                        if wanted:
                            slot = slots[u][kind, i]
                            unit(kind, i, n, u if kind in "TK" else 1 - u, slot, held[slot])
                            held[slot] = (kind, i, n)

                    for t in range(KT):
                        score(b, t, u)
                        for kind, i in plans[u][t]:
                            go(kind, i)
                        if t:
                            pv(b, t - 1, u)
                    go("K", 0)
                    pv(b, KT - 1, u)
                    go("K", 1)
                    go("K", 2)

                def prologue(kind, count, n, held):
                    for i in range(count):
                        unit(kind, i, n, n % 2, i % RING, held[i % RING])
                        held[i % RING] = (kind, i, n)

                pe.wait_ge(init, INIT)
                pe.wait_ge(pack_rest, 16)
                pe.wait_ge(split_done, 2)
                held = [None] * RING
                prologue("T", 3, 0, held)
                out_projection(QUADS - 1)
                prologue("K", 3, 0, held)
                x1_T(QUADS - 1)
                prologue("V", 3, 0, held)
                queries(QUADS - 1)
                prologue("M", NM, 0, held)
                prologue("T", 3, 1, held)
                prologue("K", 3, 1, held)
                pe.wait_ge(ql_done, QUADS)
                nc.tensor.matmul(banks[1][0:1, 0:P], w("bv"), w("WoT"), start=True, stop=True).then_inc(row_ps, 1)
                pe.wait_ge(row_done, 3)
                pe.wait_ge(o_zeroed, 1)
                for b in range(2):
                    body(b, 0, b % 2, True, True, False)
                with pe.Fori(1, B // 2 - 1) as i:
                    for u in range(2):
                        body(i * 2 + u, i, u, True, True, u == 0)
                for b in range(B - 2, B):
                    body(b, b // 2, b % 2, b + 2 < B, b + 1 < B, b % 2 == 0)
                for k, (kind, i) in enumerate(EPILOGUE):
                    unit(kind, i, B // 2 - 1, 0, k, ("M", NM - 1, B - 1))

            @block.vector
            def _(dve):
                dve.memset(c_hl[96:P, :, :], 0.0).then_inc(init, 1)
                dve.wait_ge(row_ps, 1)
                dve.tensor_copy(b_all[:, :], banks[4][:, 0:P]).then_inc(row_done, 1)
                dve.tensor_copy(b2_all[:, :], banks[4][:, P:2 * P]).then_inc(row_done, 1)

                def feature_min(q, u):
                    dve.wait_ge(feat_exp, q * 8 + u + 1)
                    dve.tensor_scalar(e_buf[:, u % 4, :], e_buf[:, u % 4, :], 1.0, None, ALU.min).then_inc(feat_min, 1)

                def feature(q, u):
                    dve.wait_ge(feat_min, q * 8 + u + 1)
                    dst = kf[:, u, :] if u < 4 else qf[:, u - 4, :]
                    dve.scalar_tensor_tensor(dst, banks[2 + u % 4], 0.0, e_buf[:, u % 4, :], ALU.max,
                                             ALU.add).then_inc(feat_done, 1)

                def features(q, us):
                    feature_min(q, us[0])
                    for u in us:
                        if u + 1 in us:
                            feature_min(q, u + 1)
                        feature(q, u)

                def residual(q):
                    dve.wait_ge(yo_ps, q + 1)
                    dve.wait_ge(xres_ready, q + 1)
                    dve.tensor_tensor(xr[:, :], YO, xres[:, :], ALU.add).then_inc(xr_done, 1)
                    dve.wait_ge(xr_done, q + 1)
                    ln_stats(dve, xr, stats, mv, (ln1_stats, ln1_var, dve_settled), q)

                def normalise(q):
                    wait_past(dve, x1_kept, q)
                    ln_apply(dve, xr, x1, mv, std, rstd, ln1_std, ln1_rstd, q).then_inc(x1_done, 1)

                def key_values(q):
                    for i in range(2):
                        dve.wait_ge(kv_ps, q * 2 + i + 1)
                        src = psum[:, 6:8, 0:8 * KVW].rearrange("p e (a c) -> p e a c", a=8)
                        dve.tensor_tensor(kvn[:, i, :, :, :], src[:, :, :, 0:32], mask_kv, ALU.mult)
                        dve.tensor_tensor(kvd[:, i, :, :, :], src[:, :, :, 32:33].to_broadcast([P, 2, 8, 32]), mask_kv,
                                          ALU.mult).then_inc(kv_sb, 1)

                def q_lo(q):
                    dve.wait_ge(qh_done, q + 1)
                    dve.scalar_tensor_tensor(ql[:, bass.ds(q * QT, QT)], banks[1], w("bq"),
                                             qh[:, bass.ds(q * QT, QT)], ALU.add, ALU.subtract).then_inc(ql_done, 1)

                def attend(q):
                    dve.wait_ge(den_done, q + 1)
                    dve.reciprocal(rden[:, :], den[:, :]).then_inc(rden_done, 1)
                    dve.wait_ge(rden_done, q + 1)
                    dve.tensor_tensor(aT[:, :], banks[2], rden[:, :], ALU.mult).then_inc(aT_done, 1)

                def front(q, back):
                    features(q, range(0, 2))
                    if back:
                        residual(q - 1)
                    features(q, range(2, 4))
                    if back:
                        normalise(q - 1)
                    features(q, range(4, 8))
                    key_values(q)
                    if back:
                        q_lo(q - 1)
                    attend(q)

                front(0, False)
                dve.wait_ge(pack_rest, 16)
                for name, hi in (("WkT", WkH), ("WvT", WvH)):
                    dve.tensor_copy(hi[:, :], w(name)).then_inc(split_hi, 1)
                dve.tensor_copy(ident16[:, :], ident).then_inc(init, 1)
                dve.wait_ge(split_hi, 2)
                for name, hi, lo in (("WkT", WkH, WkL), ("WvT", WvH, WvL)):
                    dve.tensor_tensor(lo[:, :], w(name), hi[:, :], ALU.subtract).then_inc(split_done, 1)
                for t in k_stack:
                    dve.memset(t[96:97, :, :], SHIFT).then_inc(init, 1)
                    dve.memset(t[0:96, :, S:S + 4], 0.0).then_inc(init, 1)
                dve.memset(o_n[:, :, :, :], 0.0).then_inc(init, 1)

                steps = [0]

                def chain(ins):
                    ins.then_inc(c_step, 1)
                    steps[0] += 1
                    dve.wait_ge(c_step, steps[0])

                theta = w("theta")
                n, f0, f1, sn, cs = (ang[:, i, :] for i in range(5))
                chain(dve.tensor_scalar(n, theta, INV2PI, None, ALU.mult))
                chain(dve.tensor_scalar(n, n, ROUND, -ROUND, ALU.add, ALU.add))
                chain(dve.scalar_tensor_tensor(theta_r[:, :], n, -C1, theta, ALU.mult, ALU.add))
                chain(dve.scalar_tensor_tensor(theta_r[:, :], n, -C2, theta_r[:, :], ALU.mult, ALU.add))
                chain(dve.scalar_tensor_tensor(theta_r[:, :], n, -C3, theta_r[:, :], ALU.mult, ALU.add))
                chain(dve.tensor_scalar(f0, theta_r[:, :], INV2PI, None, ALU.mult))
                chain(dve.scalar_tensor_tensor(u_bias[:, :], w("b1"), 0.1 * INV2PI, f0, ALU.mult, ALU.add))
                chain(dve.tensor_scalar(f0, f0, 0.5, -0.5, ALU.min, ALU.max))
                chain(dve.tensor_scalar(f1, f0, 0.25, None, ALU.add))
                chain(dve.tensor_scalar(n, f1, ROUND, -ROUND, ALU.add, ALU.add))
                dve.tensor_tensor(f1, f1, n, ALU.subtract).then_inc(turns_in, 1)

                front(1, True)
                with dve.Fori(2, QUADS) as q:
                    front(q, True)

                def t_copy(n, i, bank):
                    dve.wait_ge(ready["T"], n * 3 + i + 1)
                    if i == 0:
                        wait_past(dve, ready["V"], n * 3)
                        wait_past(dve, ready["K"], n * 3)
                    dve.tensor_copy(cT[:, i * TPB:(i + 1) * TPB, :],
                                    bank.bitcast(F16).rearrange("p (t k) -> p t k", t=TPB)).then_inc(cT_done, 1)

                def k_lo(n, i):
                    dve.wait_ge(kh_done, n * 3 + i + 1)
                    if i == 0:
                        wait_past(dve, k_stacked, n * 192)
                    dve.scalar_tensor_tensor(kl[:, i * CH:(i + 1) * CH], ring[i][:, 0:CH], w("bk"),
                                             kh[:, i * CH:(i + 1) * CH], ALU.add, ALU.subtract).then_inc(kl_done, 1)

                def m_max(n, i, bank):
                    dve.wait_ge(ready["M"], n * NM + i + 1)
                    if i == 0:
                        wait_past(dve, m_fold, n)
                    dve.tensor_reduce(mx[:, i:i + 1], bank[:, 0:CH], AX.X, ALU.max).then_inc(mx_done, 1)

                def m_row(n):
                    dve.wait_ge(mx_done, (n + 1) * NM)
                    dve.tensor_reduce(mrow[:, :], mx[:, :].rearrange("p (r c) -> p r c", c=KC), AX.X,
                                      ALU.max).then_inc(m_fold, 1)
                    dve.wait_ge(m_fold, n + 1)
                    dve.tensor_scalar(m16[:, 0:MB], mrow[:, :], -1.0 / SHIFT, None, ALU.mult).then_inc(m_cast, 1)
                    dve.wait_ge(m_cast, n + 1)
                    wait_past(dve, m_placed, n * 64)
                    dve.transpose(mT[:, :], m16[:, :]).then_inc(m_ready, 1)

                def invert(pair, i, bank):
                    dve.wait_ge(ready["R"], pair * 2 + i + 1)
                    lo, n = (0, 3 * N) if i == 0 else (3 * N, N)
                    dve.reciprocal(r_sb[:, :, lo:lo + n], bank[:, 0:2 * n].rearrange("p (e n) -> p e n", e=2)
                                   ).then_inc(r_inv, 1)

                def scale_o(pair):
                    dve.wait_ge(r_inv, pair * 2 + 2)
                    dve.tensor_tensor(o_n[:, :, :, 0:N].rearrange("p s e n -> p e s n"),
                                      o_sb[:, :, :].rearrange("p e (s n) -> p e s n", s=4),
                                      r_sb[:, :, :].rearrange("p e (s n) -> p e s n", s=4),
                                      ALU.mult).then_inc(o_ready, 1)

                def add_y(pair, bank):
                    dve.wait_ge(ready["Y"], pair + 1)
                    xs = x_pairs[:, bass.ds(pair, 1), :].rearrange("p o d -> p (o d)")
                    dve.tensor_tensor(xs, bank[:, 0:D], xs, ALU.add).then_inc(y_added, 1)

                def o_copy(b, pair, u):
                    dve.wait_ge(pv_done, b * KT + KT)
                    if u == 0:
                        wait_past(dve, ready["R"], pair * 2)
                        wait_past(dve, o_ready, pair)
                    dve.tensor_copy(o_sb[:, u, :], O[:, 0:GC]).then_inc(o_copied, 1)

                for i in range(3):
                    t_copy(0, i, ring[i])
                residual(QUADS - 1)
                normalise(QUADS - 1)
                for i in range(3):
                    k_lo(0, i)
                dve.wait_ge(xr_done, QUADS)
                dve.memset(O, 0.0).then_inc(o_zeroed, 1)
                q_lo(QUADS - 1)
                for i in range(NM):
                    m_max(0, i, ring[i % RING])
                m_row(0)
                for i in range(3):
                    t_copy(1, i, ring[i])
                for i in range(3):
                    k_lo(1, i)
                dve.wait_ge(sin_done, 1)
                chain(dve.tensor_tensor(ang[:, 5, :], cs, w("wr"), ALU.mult))
                chain(dve.tensor_tensor(ang[:, 6, :], sn, w("wi"), ALU.mult))
                chain(dve.tensor_tensor(ang[:, 5, :], ang[:, 5, :], ang[:, 6, :], ALU.add))
                chain(dve.scalar_tensor_tensor(s_coef[:, :], ang[:, 5, :], 0.1, w("wi"), ALU.mult, ALU.mult))
                dve.wait_ge(row_ps, 2)
                dve.tensor_tensor(wslots[0:1, 0, :], banks[1][0:1, 0:P], m["bo_row"], ALU.add).then_inc(row_done, 1)

                def body(b, pair, u, s1, s2, epilogue):
                    for t in range(KT):
                        for kind, i in plans[u][t]:
                            if kind in "MTRY":
                                bank = ring[slots[u][kind, i]]
                            if kind == "M" and s2:
                                m_max(b + 1, i, bank)
                                if i == NM - 1:
                                    m_row(b + 1)
                            if kind == "T" and s1:
                                t_copy(b + 2, i, bank)
                            if kind == "R" and epilogue:
                                invert(pair - 1, i, bank)
                                if i == 1:
                                    scale_o(pair - 1)
                            if kind == "Y" and epilogue:
                                add_y(pair - 1, bank)
                    if s1:
                        k_lo(b + 2, 0)
                    o_copy(b, pair, u)
                    if s1:
                        k_lo(b + 2, 1)
                        k_lo(b + 2, 2)

                for b in range(2):
                    body(b, 0, b, True, True, False)
                with dve.Fori(1, B // 2 - 1) as i:
                    for u in range(2):
                        body(i * 2 + u, i, u, True, True, u == 0)
                for b in range(B - 2, B):
                    body(b, b // 2, b % 2, b + 2 < B, b + 1 < B, b % 2 == 0)
                last_pair = B // 2 - 1
                for i in range(2):
                    invert(last_pair, i, ring[i])
                scale_o(last_pair)
                add_y(last_pair, ring[2])


def ffn_block(nc, out_dram, m):
    w, banks, ident, eps, b2_all, x_all = (m[k] for k in ("w", "banks", "ident", "eps", "b2_all", "x_all"))
    with ExitStack() as stack:
        def sb(name, shape, dt=F32):
            return stack.enter_context(nc.sbuf_tensor(name, shape, dt))

        def sem(name):
            return stack.enter_context(nc.semaphore(name))

        x2 = sb("x2", [P, 4 * D])
        x2b = sb("x2b", [P, 4 * D])
        x2T = sb("x2T", [P, QT])
        turns = sb("turns", [P, 2, QT])
        whole = sb("whole", [P, 2, QT])
        frac = sb("frac", [P, 2, QT])
        sine = sb("sine", [P, 2, QT])
        z = sb("z", [P, 2, QT])
        hid = sb("hid", [P, G, QT])
        y = sb("y", [P, 4 * D])
        out_t = sb("out_t", [P, 4 * D])
        stats = [sb(f"stats{i}", [P, 4, 6]) for i in (2, 3)]
        mv = [sb(f"mv{i}", [P, 4, 2]) for i in (2, 3)]
        std = [sb(f"std{i}", [P, 4]) for i in (2, 3)]
        rstd = [sb(f"rstd{i}", [P, 4]) for i in (2, 3)]
        x2_done, x2b_done, x2T_ps, x2T_sb, h_ps = (sem("x2_done"), sem("x2b_done"), sem("x2T_ps"), sem("x2T_sb"),
                                                   sem("h_ps"))
        turns_ready, whole_ready, frac_ready, sine_ready = (sem("turns_ready"), sem("whole_ready"),
                                                            sem("frac_ready"), sem("sine_ready"))
        z_ready, hid_ready, f_ps, y_done, out_ready, stored = (sem("z_ready"), sem("hid_ready"), sem("f_ps"),
                                                               sem("y_done"), sem("out_ready"), sem("stored"))
        ln_sems = [[sem(f"ln{k}_{what}") for what in ("stats", "var", "std", "rstd")] for k in (2, 3)]
        sp_settled, dve_settled = sem("sp_settled3"), sem("dve_settled3")
        W1 = w("W1")
        W2 = w("W2").rearrange("p (g n) -> p g n", g=G)
        out_view = out_dram.rearrange("(q p e) n d -> q e n p d", q=QUADS, e=2)

        with nc.Block() as block:
            @block.sync
            def _(sp):
                with sp.Fori(0, QUADS) as q:
                    sp.wait_ge(out_ready, q + 1)
                    settle(sp, sp_settled)
                    for e in range(2):
                        dst = out_view[bass.ds(q, 1), e, :, :, :].rearrange("o n p d -> n (o p) d")
                        sp.dma_start(dst, out_t[SLOT * e:SLOT * e + N, :].rearrange("r (p d) -> r p d", p=4)
                                     ).then_inc(stored, 16)
                sp.wait_ge(stored, QUADS * 32)

            @block.gpsimd
            def _(pool):
                def add_b2(q):
                    pool.wait_ge(x2_done, q + 1)
                    wait_past(pool, y_done, q)
                    nc.gpsimd.tensor_tensor(
                        x2b[:, :].rearrange("p (a d) -> p a d", a=4), x2[:, :].rearrange("p (a d) -> p a d", a=4),
                        b2_all[:, :].rearrange("p (o d) -> p o d", o=1).to_broadcast([P, 4, D]),
                        ALU.add).then_inc(x2b_done, 1)

                def fractions(q):
                    for g in range(G):
                        pool.wait_ge(whole_ready, q * G + g + 1)
                        wait_past(pool, sine_ready, q * G + g - 1)
                        nc.gpsimd.tensor_tensor(frac[:, g % 2, :], turns[:, g % 2, :], whole[:, g % 2, :],
                                                ALU.subtract).then_inc(frac_ready, 1)

                add_b2(0)
                fractions(0)
                with pool.Fori(1, QUADS) as q:
                    add_b2(q)
                    fractions(q)

            @block.scalar
            def _(act):
                def root(k, q):
                    act.wait_ge(ln_sems[k][1], q + 1)
                    nc.scalar.activation(std[k][:, :], mv[k][:, :, 1], ACT.Sqrt,
                                         bias=eps[:, 0:1]).then_inc(ln_sems[k][2], 1)

                def turn(q, g):
                    act.wait_ge(h_ps, q * G + g + 1)
                    wait_past(act, frac_ready, q * G + g - 1)
                    nc.scalar.activation(turns[:, g % 2, :], banks[2 + g], ACT.Identity,
                                         bias=m["u_bias"][:, g:g + 1], scale=0.1 * INV2PI).then_inc(turns_ready, 1)

                def relu(q, g):
                    act.wait_ge(z_ready, q * G + g + 1)
                    if g == 0:
                        wait_past(act, f_ps, q)
                    nc.scalar.activation(hid[:, g, :], z[:, g % 2, :], ACT.Relu,
                                         bias=w("b1")[:, g:g + 1]).then_inc(hid_ready, 1)

                def step(q, front, back):
                    if back:
                        root(1, q - 1)
                    if front:
                        root(0, q)
                        act.wait_ge(x2T_ps, q + 1)
                        nc.scalar.copy(x2T[:, :], banks[0]).then_inc(x2T_sb, 1)
                        turn(q, 0)
                        turn(q, 1)
                        for g in range(G):
                            act.wait_ge(frac_ready, q * G + g + 1)
                            wait_past(act, z_ready, q * G + g - 1)
                            nc.scalar.activation(sine[:, g % 2, :], frac[:, g % 2, :], ACT.Sin,
                                                 scale=TWO_PI_BELOW).then_inc(sine_ready, 1)
                            if g + 2 < G:
                                turn(q, g + 2)
                            if g:
                                relu(q, g - 1)
                        relu(q, G - 1)

                step(0, True, False)
                with act.Fori(1, QUADS) as q:
                    step(q, True, True)
                step(QUADS, False, True)

            @block.tensor
            def _(pe):
                def front(q):
                    pe.wait_ge(x2_done, q + 1)
                    for p in range(4):
                        last = nc.tensor.transpose(banks[0][:, p * P:(p + 1) * P], x2[:, p * D:(p + 1) * D], ident)
                    last.then_inc(x2T_ps, 1)
                    pe.wait_ge(x2T_sb, q + 1)
                    for g in range(G):
                        wait_past(pe, z_ready, q * G - G + g + 1)
                        nc.tensor.matmul(banks[2 + g], W1[:, g * P:(g + 1) * P], x2T[:, :], start=True,
                                         stop=True).then_inc(h_ps, 1)

                def back(q):
                    pe.wait_ge(hid_ready, (q + 1) * G)
                    for p in range(4):
                        for g in range(G):
                            last = nc.tensor.matmul(banks[1][:, p * P:(p + 1) * P], hid[:, g, p * P:(p + 1) * P],
                                                    W2[:, g, :], start=(g == 0), stop=(g == G - 1))
                    last.then_inc(f_ps, 1)

                front(0)
                with pe.Fori(1, QUADS) as q:
                    back(q - 1)
                    front(q)
                back(QUADS - 1)

            @block.vector
            def _(dve):
                def stats2(q):
                    xs = x_all[:, bass.ds(q, 1), :].rearrange("p o n -> p (o n)")
                    ln_stats(dve, xs, stats[0], mv[0], (ln_sems[0][0], ln_sems[0][1], dve_settled), q)

                def apply2(q):
                    xs = x_all[:, bass.ds(q, 1), :].rearrange("p o n -> p (o n)")
                    wait_past(dve, x2T_ps, q)
                    wait_past(dve, x2b_done, q)
                    ln_apply(dve, xs, x2, mv[0], std[0], rstd[0], ln_sems[0][2], ln_sems[0][3], q
                             ).then_inc(x2_done, 1)

                def sum3(q):
                    dve.wait_ge(f_ps, q + 1)
                    dve.wait_ge(x2b_done, q + 1)
                    dve.tensor_tensor(y[:, :], banks[1], x2b[:, :], ALU.add).then_inc(y_done, 1)
                    dve.wait_ge(y_done, q + 1)
                    ln_stats(dve, y, stats[1], mv[1], (ln_sems[1][0], ln_sems[1][1], dve_settled), q)

                def apply3(q):
                    wait_past(dve, stored, q * 32)
                    ln_apply(dve, y, out_t, mv[1], std[1], rstd[1], ln_sems[1][2], ln_sems[1][3], q
                             ).then_inc(out_ready, 1)

                def modulate(q):
                    def rounded(g):
                        dve.wait_ge(turns_ready, q * G + g + 1)
                        wait_past(dve, frac_ready, q * G + g - 1)
                        dve.tensor_scalar(whole[:, g % 2, :], turns[:, g % 2, :], ROUND, -ROUND, ALU.add,
                                          ALU.add).then_inc(whole_ready, 1)

                    rounded(0)
                    rounded(1)
                    for g in range(G):
                        dve.wait_ge(sine_ready, q * G + g + 1)
                        wait_past(dve, hid_ready, q * G + g - 1)
                        dve.scalar_tensor_tensor(z[:, g % 2, :], sine[:, g % 2, :], m["s_coef"][:, g:g + 1],
                                                 banks[2 + g], ALU.mult, ALU.add).then_inc(z_ready, 1)
                        if g + 2 < G:
                            rounded(g + 2)

                def step(q):
                    stats2(q)
                    sum3(q - 1)
                    apply2(q)
                    apply3(q - 1)
                    modulate(q)

                stats2(0)
                apply2(0)
                modulate(0)
                step(1)
                with dve.Fori(2, QUADS) as q:
                    step(q)
                sum3(QUADS - 1)
                apply3(QUADS - 1)


def pack_inputs(i):
    t = {name: np.zeros((P, width), np.float32) for name, (_, width) in PACK.items()}
    f = {k: np.asarray(v) for k, v in i.items()}
    part = np.arange(P)
    t["ident"][part, part] = 1
    wqkv = f["L0_attn_w_qkv"]
    t["wqT"][:], t["wkT"][:], t["wv"][:] = wqkv[:, 0:D].T, wqkv[:, D:2 * D].T, wqkv[:, 2 * D:]
    for h in range(H):
        t["proj"][h * HD:(h + 1) * HD, h * FEAT:(h + 1) * FEAT] = f["L0_attn_proj_matrix"][h]
    t["w_out"][:] = f["L0_attn_w_out"]
    for name in ("Wq", "Wk", "Wv", "Wo"):
        t[name + "T"][:] = f["L0_xattn_" + name].T
    for h in range(H):
        j, s = divmod(h, 4)
        at = 32 * j + (8 + 8 * s if s < 3 else 0)
        t["WoSlots"][at:at + HD, s * P:(s + 1) * P] = f["L0_xattn_Wo"].T[h * HD:(h + 1) * HD]
    t["selA"][32 * (part // 32), part] = 1
    t["selB"][32 * (part // 32) + 8, part] = 1
    for h in range(4):
        t["maskKV"][32 * h:32 * h + 32, 8 * h:8 * h + 8] = 1
    for h in range(4):
        t["maskQ"][part % 32 // HD == h, h] = 1
    for h in range(H):
        t["maskM"][part // HD == h, h] = 1
    t["W1"][:] = f["L0_ffn_W1"]
    t["W2"][:] = f["L0_ffn_W2"].reshape(4, P, D).transpose(1, 0, 2).reshape(P, 4 * D)
    for name, key in (("bq", "L0_xattn_bq"), ("bk", "L0_xattn_bk"), ("bv", "L0_xattn_bv")):
        t[name][:, 0] = f[key]
    for name, key in (("b1", "L0_ffn_b1"), ("theta", "L0_ffn_quantum_phases"),
                      ("wr", "L0_ffn_quantum_weights_real"), ("wi", "L0_ffn_quantum_weights_imag")):
        t[name][:] = f[key].reshape(4, P).T
    for n, key in enumerate(("L0_attn_b_out", "L0_xattn_bo", "L0_ffn_b2")):
        t["rows"][0, n * P:(n + 1) * P] = f[key]
    return np.ascontiguousarray(np.concatenate([t[name] for name in PACK], axis=1))


def kernel(**inputs):
    import concourse.bacc as bacc
    from concourse.bass_utils import run_bass_kernel_spmd

    nc = bacc.Bacc("TRN2", target_bir_lowering=False, num_devices=1)
    arrays = {"ctx_in": np.ascontiguousarray(inputs["ctx_1024"]), "x_in": np.ascontiguousarray(inputs["x"]),
              "pack_in": pack_inputs(inputs)}
    drams = [nc.dram_tensor(name, a.shape, F32, kind="ExternalInput").ap() for name, a in arrays.items()]
    out = nc.dram_tensor("out", (B, N, D), F32, kind="ExternalOutput").ap()
    build(nc, *drams, out)
    return run_bass_kernel_spmd(nc, [arrays], core_ids=[0]).results[0]["out"]
```

```python
from contextlib import ExitStack

import numpy as np

import concourse.bass as bass
from concourse import mybir

F32 = mybir.dt.float32
F16 = mybir.dt.float16
ALU = mybir.AluOpType
ACT = mybir.ActivationFunctionType
AX = mybir.AxisListType

P = 128
B, N, D = 32, 56, 128
S = 1500
H, HD = 16, 8
FEAT = 32
FF = 512
SLOT = 64
QUADS = B // 8
QT = 8 * SLOT
G = 4
GC = 4 * N
HQ = H * N
KP = 125
KT = S // KP
KC = 3
CH = S // KC
MB = HQ // P
NM = MB * KC
ROWS = 97
SHIFT = 64.0
PBUF = 4
RING = 3
KVW = 33
SCALE = float(HD) ** -0.5
EPS = 1e-5
ROUND = 1.5 * 2.0 ** 23
INV2PI = float(1.0 / (2.0 * np.pi))
TWO_PI_BELOW = 6.283185
C1 = 6.28125
C2 = 0.0019350051879882812
C3 = float(2.0 * np.pi - C1 - C2)

PACK = {}
_at = 0
for _name, _w in (("ident", P), ("wqT", P), ("wkT", P), ("wv", P), ("proj", H * FEAT), ("w_out", P),
                  ("WqT", P), ("bq", 1), ("maskKV", 32), ("rows", 3 * P),
                  ("WkT", P), ("WvT", P), ("WoT", P), ("WoSlots", 4 * P), ("selA", P),
                  ("selB", P), ("maskQ", 4), ("maskM", H), ("W1", FF), ("W2", FF),
                  ("bk", 1), ("bv", 1), ("b1", 4), ("theta", 4), ("wr", 4), ("wi", 4)):
    PACK[_name] = (_at, _w)
    _at += _w
PACKW = _at
PACK_FIRST = PACK["WkT"][0]


def wait_past(engine, semaphore, count):
    if not isinstance(count, int) or count > 0:
        engine.wait_ge(semaphore, count)


def settle(engine, counter):
    engine.nop().then_inc(counter, 1)


STORE_ORDER = (0, 1, 3, 2)
END_SLOT = 2
X2T_STEPS = (2, 4, 6)
FBUF = 4
PROJECT_LAG = 5
AHEAD = 2
ROOT_UNIT = 4
M_COUNTS = (2, 2, 3, 2, 3, 2, 3, 2, 2)
V_STEPS, T_STEPS, Y_STEP = (0, 2, 4), (8, 9, 10), 6
T1_AFTER = (10, 12, 14)
X_STEP = 11
TAIL = [("K", c) for c in range(KC)]


def unit_plan(u):
    steps = [[] for _ in range(KT)]
    m = 0
    for t, count in enumerate(M_COUNTS, start=1):
        for _ in range(count):
            steps[t].append(("M", m))
            m += 1
    for i, t in enumerate(V_STEPS):
        steps[t].append(("V", i))
    for i, t in enumerate(T_STEPS):
        steps[t].append(("T", i))
    steps[X_STEP].append(("X", 0))
    steps[0].insert(0, ("R", 0))
    if u == 0:
        steps[Y_STEP].insert(0, ("Y", 0))
    return steps


def ring_slots():
    rounds = [[unit for step in unit_plan(u) for unit in step] + TAIL for u in range(2)]
    first, second = len(rounds[0]), len(rounds[1])
    skip = -(first + second) % RING
    return [{unit: k % RING for k, unit in enumerate(rounds[0])},
            {unit: (first + k + (skip if unit in TAIL else 0)) % RING for k, unit in enumerate(rounds[1])}]


def early_bank(kind, i):
    if kind == "K1":
        return 4 + i
    order = [("T", c) for c in range(KC)] + [("K", c) for c in range(KC)] + [("V", c) for c in range(KC)]
    for j in range(NM):
        order += [("M", j)] + ([("T1", T1_AFTER.index(j))] if j in T1_AFTER else [])
    return 2 + (order + [("X", 0)]).index((kind, i)) % 4


def build(nc, ctx_dram, x_dram, pack_dram, out_dram):
    with ExitStack() as stack:
        pack = stack.enter_context(nc.sbuf_tensor("pack", [P, PACKW], F32))

        def w(name):
            at, width = PACK[name]
            return pack[:, at:at + width]

        row_at = PACK["rows"][0]
        shared = {
            "pack": pack, "w": w, "ident": w("ident"), "wslots": w("WoSlots").rearrange("p (s n) -> p s n", s=4),
            "b_out_row": pack[0:1, row_at:row_at + P],
            "bo_row": pack[0:1, row_at + P:row_at + 2 * P],
            "b2_row": pack[0:1, row_at + 2 * P:row_at + 3 * P],
        }
        for name, shape in (("eps", [P, 1]), ("b2_all", [P, P]), ("x_all", [P, QUADS, 4 * D]),
                            ("u_bias", [P, 4]), ("s_coef", [P, 4])):
            shared[name] = stack.enter_context(nc.sbuf_tensor(name, shape, F32))
        psum = stack.enter_context(nc.psum_tensor("psum", [P, 8, 512], F32))
        shared["psum"], shared["banks"] = psum, [psum[:, i, :] for i in range(8)]
        decoder_block(nc, ctx_dram, x_dram, pack_dram, out_dram, shared)


def ln_stats(dve, src, stats, mv, sems, q):
    stats_done, var_ready, settled = sems
    for p in range(4):
        last = dve.bn_stats(stats[:, p, :], src[:, p * D:(p + 1) * D])
    last.then_inc(stats_done, 1)
    dve.wait_ge(stats_done, q + 1)
    settle(dve, settled)
    for p in range(4):
        last = dve.bn_aggr(mv[:, p, :], stats[:, p, :])
    last.then_inc(var_ready, 1)


def ln_apply(dve, src, dst, mv, std, rstd, std_ready, rstd_ready, q):
    dve.wait_ge(std_ready, q + 1)
    dve.reciprocal(rstd[:, :], std[:, :]).then_inc(rstd_ready, 1)
    dve.wait_ge(rstd_ready, q + 1)
    for p in range(4):
        last = dve.tensor_scalar(dst[:, p * D:(p + 1) * D], src[:, p * D:(p + 1) * D],
                                 mv[:, p, 0:1], rstd[:, p:p + 1], ALU.subtract, ALU.mult)
    return last


def decoder_block(nc, ctx_dram, x_dram, pack_dram, out_dram, m):
    pack, w, ident, eps, b2_all, wslots = (m[k] for k in ("pack", "w", "ident", "eps", "b2_all", "wslots"))
    x_all, psum, banks, u_bias, s_coef = (m[k] for k in ("x_all", "psum", "banks", "u_bias", "s_coef"))
    x_pairs = x_all[:, :, :].rearrange("p q (a d) -> p (q a) d", a=4)
    TPB = 8
    slots = ring_slots()
    plans = [unit_plan(0), unit_plan(1)]

    with ExitStack() as stack:
        def sb(name, shape, dt=F32):
            return stack.enter_context(nc.sbuf_tensor(name, shape, dt))

        def sem(name):
            return stack.enter_context(nc.semaphore(name))

        wqp, wkp = sb("wqp", [P, H * FEAT]), sb("wkp", [P, H * FEAT])
        WkH, WkL = sb("WkH", [P, P], F16), sb("WkL", [P, P], F16)
        WvH, WvL = sb("WvH", [P, P], F16), sb("WvL", [P, P], F16)
        ones = sb("ones", [P, P])
        eps_z = sb("eps_z", [P, 1])
        b_all = sb("b_all", [P, P])
        xq = sb("xq", [P, 4 * D])
        xres = sb("xres", [P, 4 * D])
        xT = sb("xT", [P, QT])
        e_buf = sb("e_buf", [P, 4, 512])
        kf = sb("kf", [P, 4, H * FEAT])
        qf = sb("qf", [P, G, QT])
        v_s = sb("v_s", [P, 4 * G, 2, KVW])
        kvn = sb("kvn", [P, 2, 2, 8, 32])
        kvd = sb("kvd", [P, 2, 2, 8, 32])
        den = sb("den", [P, QT])
        rden = sb("rden", [P, QT])
        aT = sb("aT", [P, QT])
        xr = sb("xr", [P, 4 * D])
        x1 = sb("x1", [P, 4 * D])
        x1T = sb("x1T", [P, QT])
        qh = sb("qh", [P, B * SLOT], F16)
        ql = sb("ql", [P, B * SLOT], F16)
        q_stack = sb("q_stack", [96, G, B * SLOT], F16)
        stats, mv = sb("stats", [P, 4, 6]), sb("mv", [P, 4, 2])
        std, rstd = sb("std", [P, 4]), sb("rstd", [P, 4])
        ang = sb("ang", [P, 8, 4])
        theta_r = sb("theta_r", [P, 4])

        pack_first, pack_rest, x_zeroed = sem("pack_first"), sem("pack_rest"), sem("x_zeroed")
        x_first, x_rest, consts = sem("x_first"), sem("x_rest"), sem("consts")
        v_zeros, v_ones, c_zeroed = sem("v_zeros"), sem("v_ones"), sem("c_zeroed")
        fold_ps, fold_sb, row_ps, row_done = sem("fold_ps"), sem("fold_sb"), sem("row_ps"), sem("row_done")
        split_hi, split_done = sem("split_hi"), sem("split_done")
        c_step, turns_in, sin_done = sem("c_step"), sem("turns_in"), sem("sin_done")
        xq_ready, xres_ready, xT_ps, xT_sb = sem("xq_ready"), sem("xres_ready"), sem("xT_ps"), sem("xT_sb")
        feat_ps, feat_act, feat_done = sem("feat_ps"), sem("feat_act"), sem("feat_done")
        v_ps, v_sb, kv_ps, kv_sb = sem("v_ps"), sem("v_sb"), sem("kv_ps"), sem("kv_sb")
        at_ps, den_done, rden_done, aT_done = sem("at_ps"), sem("den_done"), sem("rden_done"), sem("aT_done")
        yo_ps, xr_done = sem("yo_ps"), sem("xr_done")
        ln1_stats, ln1_var, ln1_std, ln1_rstd = sem("ln1_stats"), sem("ln1_var"), sem("ln1_std"), sem("ln1_rstd")
        x1_done, x1_kept = sem("x1_done"), sem("x1_kept")
        x1T_ps, x1T_sb, q_ps, qh_done, ql_done = (sem("x1T_ps"), sem("x1T_sb"), sem("q_ps"), sem("qh_done"),
                                                  sem("ql_done"))
        q_stacked = sem("q_stacked")
        sp_settled, pool_settled, dve_settled = sem("sp_settled"), sem("pool_settled"), sem("dve_settled")
        mask_kv = w("maskKV").rearrange("p (e a c) -> p e a c", e=1, a=1).to_broadcast([P, 2, 8, 32])
        x_view = x_dram.rearrange("(a e) n d -> e n a d", e=2)

        c_in = sb("c_in", [P, 2, KT * D])
        c_hl = sb("c_hl", [P, 2 * KT, D], F16)
        cT = sb("cT", [P, 2 * KT, P], F16)
        kh, kl = sb("kh", [P, S], F16), sb("kl", [P, S], F16)
        k_stack = [sb(f"k_stack{i}", [P, G, S + 4], F16) for i in range(2)]
        q_diag = [sb(f"q_diag{i}", [P, HQ], F16) for i in range(2)]
        q_max = [sb(f"q_max{i}", [P, HQ], F16) for i in range(2)]
        v_ext = [sb(f"v_ext{i}", [P, KT, G, 48]) for i in range(2)]
        probs = sb("probs", [P, PBUF, HQ])
        mx = sb("mx", [P, NM])
        mrow = sb("mrow", [P, MB])
        m16, mT = sb("m16", [P, MB], F16), sb("mT", [MB, P], F16)
        ident16 = sb("ident16", [P, P], F16)
        o_sb = sb("o_sb", [P, 2, GC])
        r_sb = sb("r_sb", [P, 2, GC])
        o_n = sb("o_n", [P, 4, 2, SLOT])

        c_loaded, c_hi, c_split = [sem("c_loaded0"), sem("c_loaded1")], sem("c_hi"), sem("c_split")
        ready = {k: sem(f"unit_{k}") for k in "TKVMXRY"}
        cT_done, kh_done, kl_done, v_done, mx_done = (sem("cT_done"), sem("kh_done"), sem("kl_done"),
                                                      sem("v_done"), sem("mx_done"))
        m_fold, m_cast, m_ready, m_placed = sem("m_fold"), sem("m_cast"), sem("m_ready"), sem("m_placed")
        qd_ready, qm_ready, k_stacked = sem("qd_ready"), sem("qm_ready"), sem("k_stacked")
        s_ready, p_ready, pv_done = sem("s_ready"), sem("p_ready"), sem("pv_done")
        o_copied, r_inv, o_ready, y_added = sem("o_copied"), sem("r_inv"), sem("o_ready"), sem("y_added")
        init, o_zeroed = sem("init"), sem("o_zeroed")
        INIT = 2 + 6

        relu_buf = probs[:, :, :].rearrange("p b n -> p (b n)")[:, 0:4 * 512].rearrange("p (u n) -> p u n", u=4)

        x2T = kf
        hid = [qf, probs[:, :, :].rearrange("p b n -> p (b n)")[:, 0:G * QT].rearrange("p (g n) -> p g n", g=G)]
        turns = e_buf
        whole = c_in[:, :, :].rearrange("p b (k n) -> p (b k) n", n=QT)[:, 0:FBUF, :]
        sine, z = (t[:, :, :].rearrange("p g n -> p (g n)").bitcast(F32)[:, 0:FBUF * QT].rearrange(
            "p (f n) -> p f n", f=FBUF) for t in k_stack)
        stats_f, mv_f = sb("stats_f", [P, 4 * QUADS, 6]), sb("mv_f", [P, 2, 4 * QUADS, 2])
        std_f, rstd_f = sb("std_f", [P, 2, 4 * QUADS]), sb("rstd_f", [P, 2, 4 * QUADS])
        ln_stats_done, ln_var, ln_std, ln_rstd = ([sem(f"ln{k}_{what}") for k in (2, 3)]
                                                  for what in ("stats", "var", "std", "rstd"))
        x2_done, x2T_ps, x2T_sb, x2b_done, h_ps = (sem("x2_done"), sem("x2T_ps"), sem("x2T_sb"), sem("x2b_done"),
                                                   sem("h_ps"))
        turns_ready, whole_ready, frac_ready, sine_ready = (sem("turns_ready"), sem("whole_ready"),
                                                            sem("frac_ready"), sem("sine_ready"))
        z_ready, hid_ready, f_ps, y_done, out_ready, stored = (sem("z_ready"), sem("hid_ready"), sem("f_ps"),
                                                               sem("y_done"), sem("out_ready"), sem("stored"))
        UNITS = QUADS * G
        LAST = QUADS - 1
        W1, W2 = w("W1"), w("W2").rearrange("p (g n) -> p g n", g=G)
        out_view = out_dram.rearrange("(q p e) n d -> q e n p d", q=QUADS, e=2)
        X2T_BANK, F_BANKS = banks[5], (banks[4], banks[7])
        assert 4 + slots[1]["R", 0] != 5

        scores = [psum[:, 0:2, :], psum[:, 2:4, :]]
        ring = banks[4:7]
        O = banks[7]
        PER = {"T": 3, "K": 3, "V": 3, "M": NM, "X": 1, "R": 1, "Y": 1}
        DONE = {"T": cT_done, "K": kl_done, "V": v_done, "M": mx_done, "X": m_ready, "R": r_inv, "Y": y_added}

        with nc.Block() as block:
            @block.sync
            def _(sp):
                sp.dma_start(pack[:, 0:PACK_FIRST], pack_dram[:, 0:PACK_FIRST]).then_inc(pack_first, 16)
                sp.wait_ge(x_zeroed, 1)
                for e in range(2):
                    sp.dma_start(x_pairs[SLOT * e:SLOT * e + N, 0:4, :], x_view[e, :, 0:4, :]
                                 ).then_inc(x_first, 16)
                sp.dma_start(pack[:, PACK_FIRST:], pack_dram[:, PACK_FIRST:]).then_inc(pack_rest, 16)
                for e in range(2):
                    sp.dma_start(x_pairs[SLOT * e:SLOT * e + N, 4:, :], x_view[e, :, 4:, :]
                                 ).then_inc(x_rest, 16)

                def load(n, buf):
                    src = ctx_dram[bass.ds(n, 1), :, :].rearrange("o (p t) d -> p (o t d)", t=KT)
                    sp.dma_start(c_in[0:KP, buf, :], src).then_inc(c_loaded[buf], 16)

                load(0, 0)
                load(1, 1)

                def stack_q(q):
                    sp.wait_ge(ql_done, q + 1)
                    settle(sp, sp_settled)
                    wait_past(sp, q_stacked, q * 192)
                    if not isinstance(q, int):
                        settle(sp, sp_settled)
                    for c, part in enumerate((qh, ql, qh)):
                        for g in range(G):
                            sp.dma_start(q_stack[32 * c:32 * c + 32, g, bass.ds(q * QT, QT)],
                                         part[32 * g:32 * g + 32, bass.ds(q * QT, QT)]).then_inc(q_stacked, 16)

                stack_q(0)
                with sp.Fori(1, QUADS - 1) as q:
                    stack_q(q)

                def stack_k(n, u):
                    sp.wait_ge(kl_done, (n + 1) * KC)
                    settle(sp, sp_settled)
                    for c, part in enumerate((kh, kh, kl)):
                        for g in range(G):
                            sp.dma_start(k_stack[u][32 * c:32 * c + 32, g, 0:S],
                                         part[32 * g:32 * g + 32, :]).then_inc(k_stacked, 16)

                def place_m(n, u):
                    sp.wait_ge(m_ready, n + 1)
                    settle(sp, sp_settled)
                    sp.dma_start(q_diag[u][96:97, :].rearrange("o (r c) -> o r c", c=P), mT[:, :]).then_inc(m_placed, 16)

                sp.wait_ge(init, INIT)
                stack_k(0, 0)
                load(2, 0)
                sp.wait_ge(c_split, 2)
                load(3, 1)
                place_m(0, 0)
                stack_q(QUADS - 1)

                def body(b, u, stage2, load4):
                    if load4:
                        sp.wait_ge(c_split, b + 3)
                        settle(sp, sp_settled)
                        load(b + 4, u)
                    if stage2:
                        wait_past(sp, s_ready, b * KT)
                        settle(sp, sp_settled)
                        stack_k(b + 1, 1 - u)
                        place_m(b + 1, 1 - u)

                for b in range(2):
                    body(b, b, True, True)
                with sp.Fori(1, (B - 4) // 2) as i:
                    for u in range(2):
                        body(i * 2 + u, u, True, True)
                for b in range(B - 4, B):
                    body(b, b % 2, b + 1 < B, b + 4 < B)

                for count, q in enumerate(STORE_ORDER):
                    sp.wait_ge(out_ready, count + 1)
                    for e in range(2):
                        sp.dma_start(out_view[q, e, :, :, :],
                                     x_all[SLOT * e:SLOT * e + N, q, :].rearrange("r (p d) -> r p d", p=4)
                                     ).then_inc(stored, 16)
                sp.wait_ge(stored, QUADS * 32)

            @block.gpsimd
            def _(pool):
                pool.memset(x_all[:, :, :], 0.0).then_inc(x_zeroed, 1)
                for t, value in ((ones, 1.0), (eps, EPS), (eps_z, 1e-8)):
                    pool.memset(t[:], value).then_inc(consts, 1)
                for t in v_ext:
                    pool.memset(t[:, :, :, :], 1.0).then_inc(init, 1)

                def x_quad(q):
                    return x_all[:, bass.ds(q, 1), :].rearrange("p o n -> p (o n)")

                def copy_x(q):
                    if isinstance(q, int) and q == 0:
                        pool.wait_ge(x_first, 32)
                    else:
                        pool.wait_ge(x_rest, 32)
                        pool.wait_ge(xT_ps, q)
                        settle(pool, pool_settled)
                    nc.gpsimd.tensor_copy(xq[:, :], x_quad(q)).then_inc(xq_ready, 1)

                def add_b_out(q):
                    if isinstance(q, int) and q == 0:
                        pool.wait_ge(row_done, 2)
                    else:
                        pool.wait_ge(xr_done, q)
                        settle(pool, pool_settled)
                    nc.gpsimd.tensor_tensor(
                        xres[:, :].rearrange("p (a d) -> p a d", a=4), x_quad(q).rearrange("p (a d) -> p a d", a=4),
                        b_all[:, :].rearrange("p (o d) -> p o d", o=1).to_broadcast([P, 4, D]),
                        ALU.add).then_inc(xres_ready, 1)

                def keep_x1(q):
                    pool.wait_ge(x1_done, q + 1)
                    pool.wait_ge(xres_ready, q + 1)
                    settle(pool, pool_settled)
                    nc.gpsimd.tensor_copy(x_all[:, bass.ds(q, 1), :].rearrange("p o n -> p (o n)"),
                                          x1[:, :]).then_inc(x1_kept, 1)

                def split(n, buf, half):
                    pool.wait_ge(c_loaded[buf], half * 16 + 16)
                    settle(pool, pool_settled)
                    src = c_in[0:KP, buf, :].rearrange("p (t d) -> p t d", t=KT)
                    nc.gpsimd.tensor_copy(c_hl[0:KP, 0:KT, :], src).then_inc(c_hi, 1)
                    pool.wait_ge(c_hi, n + 1)
                    nc.gpsimd.tensor_tensor(c_hl[0:KP, KT:2 * KT, :], src, c_hl[0:KP, 0:KT, :],
                                            ALU.subtract).then_inc(c_split, 1)

                def diag_q(n, u):
                    q = q_stack[0:96, :, bass.ds(n * SLOT, N)].rearrange("p g (o n) -> p g o n", o=1)
                    nc.gpsimd.tensor_tensor(
                        q_diag[u][0:96, :].rearrange("p (g h n) -> p g h n", g=G, h=4),
                        q.to_broadcast([96, G, 4, N]),
                        w("maskQ")[0:96, :].rearrange("p (o h e) -> p o h e", o=1, e=1).to_broadcast([96, G, 4, N]),
                        ALU.mult).then_inc(qd_ready, 1)

                def max_q(n, u):
                    q = qh[:, bass.ds(n * SLOT, N)].rearrange("p (o n) -> p o n", o=1)
                    nc.gpsimd.tensor_tensor(
                        q_max[u][:, :].rearrange("p (h n) -> p h n", h=H), q.to_broadcast([P, H, N]),
                        w("maskM").rearrange("p (h o) -> p h o", o=1).to_broadcast([P, H, N]),
                        ALU.mult).then_inc(qm_ready, 1)

                copy_x(0)
                add_b_out(0)
                pool.wait_ge(c_zeroed, 1)
                split(0, 0, 0)
                copy_x(1)
                with pool.Fori(1, QUADS - 1) as q:
                    copy_x(q + 1)
                    add_b_out(q)
                    keep_x1(q - 1)
                add_b_out(QUADS - 1)
                keep_x1(QUADS - 2)
                pool.wait_ge(init, INIT)
                pool.wait_ge(q_stacked, 192)
                pool.wait_ge(pack_rest, 16)
                max_q(0, 0)
                diag_q(0, 0)
                pool.wait_ge(ready["T"], 3)
                split(1, 1, 0)
                max_q(1, 1)
                keep_x1(QUADS - 1)
                pool.wait_ge(ready["T"], 6)
                split(2, 0, 1)
                pool.wait_ge(q_stacked, 192 * QUADS)

                def body(b, pair, u, s1, s2, s3):
                    if s2:
                        wait_past(pool, s_ready, b * KT)
                        settle(pool, pool_settled)
                        diag_q(b + 1, 1 - u)
                    if s1:
                        pool.wait_ge(ready["M"], (b + 1) * NM)
                        settle(pool, pool_settled)
                        max_q(b + 2, u)
                    if s3:
                        pool.wait_ge(ready["T"], b * 3 + 9)
                        split(b + 3, 1 - u, pair + 1 + u)

                for b in range(2):
                    body(b, 0, b, True, True, True)
                with pool.Fori(1, (B - 4) // 2) as i:
                    for u in range(2):
                        body(i * 2 + u, i, u, True, True, True)
                for b in range(B - 4, B):
                    body(b, b // 2, b % 2, b + 2 < B, b + 1 < B, b + 3 < B)

                def add_b2(q):
                    pool.wait_ge(x2T_ps, q + 1)
                    xs = x_all[:, q, :].rearrange("p (a d) -> p a d", a=4)
                    nc.gpsimd.tensor_tensor(xs, xs, b2_all[:, :].rearrange("p (o d) -> p o d", o=1
                                                                           ).to_broadcast([P, 4, D]),
                                            ALU.add).then_inc(x2b_done, 1)

                for q in range(LAST):
                    add_b2(q)
                for k in range(UNITS):
                    pool.wait_ge(whole_ready, k + 1)
                    nc.gpsimd.tensor_tensor(turns[:, k % FBUF, :], turns[:, k % FBUF, :], whole[:, k % FBUF, :],
                                            ALU.subtract).then_inc(frac_ready, 1)
                add_b2(LAST)

            @block.scalar
            def _(act):
                for i, dst in enumerate((wqp, wkp)):
                    act.wait_ge(fold_ps, i + 1)
                    nc.scalar.copy(dst[:, :], banks[2 + i]).then_inc(fold_sb, 1)
                act.wait_ge(consts, 3)
                act.wait_ge(v_ones, 2)

                def x_T(q):
                    act.wait_ge(xT_ps, q + 1)
                    nc.scalar.copy(xT[:, :], banks[0]).then_inc(xT_sb, 1)

                def front(q, back, ahead):
                    act.wait_ge(v_ps, q + 1)
                    for e in range(2):
                        rows = slice(SLOT * e, SLOT * e + SLOT)
                        nc.scalar.copy(v_s[rows, :, e, 0:32], banks[0][rows, :].rearrange("p (a c) -> p a c", c=32)
                                       ).then_inc(v_sb, 1)
                    for u in range(8):
                        act.wait_ge(feat_ps, q * 8 + u + 1)
                        wait_past(act, feat_done, q * 8 + u - 3)
                        nc.scalar.activation(e_buf[:, u % 4, :], banks[2 + u % 4], ACT.Exp)
                        nc.scalar.activation(relu_buf[:, u % 4, :], banks[2 + u % 4], ACT.Relu).then_inc(feat_act, 1)
                    if back:
                        root(q - 1)
                    if ahead:
                        denominators(q)
                        if back:
                            x1_T(q - 1)
                        x_T(q + 1)
                        if back:
                            q_hi(q - 1)

                def denominators(q):
                    act.wait_ge(at_ps, q + 1)
                    nc.scalar.activation(den[:, :], banks[7], ACT.Identity, bias=eps_z[:, 0:1]).then_inc(den_done, 1)

                def root(q):
                    act.wait_ge(ln1_var, q + 1)
                    nc.scalar.activation(std[:, :], mv[:, :, 1], ACT.Sqrt, bias=eps[:, 0:1]).then_inc(ln1_std, 1)

                def x1_T(q):
                    act.wait_ge(x1T_ps, q + 1)
                    nc.scalar.copy(x1T[:, :], banks[1]).then_inc(x1T_sb, 1)

                def q_hi(q):
                    act.wait_ge(q_ps, q + 1)
                    nc.scalar.activation(qh[:, bass.ds(q * QT, QT)], banks[1], ACT.Identity,
                                         bias=w("bq")).then_inc(qh_done, 1)

                def exp(b, t):
                    act.wait_ge(s_ready, b * KT + t + 1)
                    wait_past(act, pv_done, b * KT + t - PBUF + 1)
                    nc.scalar.activation(probs[0:KP, t % PBUF, :].rearrange("p (a c) -> p a c", a=2),
                                         scores[t % 2][0:KP, :, 0:2 * GC], ACT.Exp, scale=SCALE).then_inc(p_ready, 1)

                def v_copy(n, i, u, bank):
                    act.wait_ge(ready["V"], n * 3 + i + 1)
                    nc.scalar.copy(v_ext[u][0:KP, 4 * i:4 * i + 4, :, 8:40],
                                   bank[0:KP, :].rearrange("p (t j c) -> p t j c", t=4, j=G)).then_inc(v_done, 1)

                def m_copy(n, bank):
                    act.wait_ge(ready["X"], n + 1)
                    wait_past(act, m_placed, n * 16)
                    nc.scalar.copy(mT[:, :], bank.bitcast(F16)[0:MB, 0:P]).then_inc(m_ready, 1)

                def k_hi(n, i, bank):
                    act.wait_ge(ready["K"], n * 3 + i + 1)
                    if i == 0:
                        wait_past(act, ready["M"], n * NM)
                        wait_past(act, k_stacked, n * 192)
                    nc.scalar.activation(kh[:, i * CH:(i + 1) * CH], bank[:, 0:CH], ACT.Identity,
                                         bias=w("bk")).then_inc(kh_done, 1)

                x_T(0)
                front(0, False, True)
                with act.Fori(1, QUADS - 1) as q:
                    front(q, True, True)
                front(QUADS - 1, True, False)
                x1_T(QUADS - 2)
                act.wait_ge(init, INIT)
                k_hi(0, 0, banks[early_bank("K", 0)])
                q_hi(QUADS - 2)
                for i in range(1, KC):
                    k_hi(0, i, banks[early_bank("K", i)])
                for i in range(KC):
                    v_copy(0, i, 0, banks[early_bank("V", i)])
                denominators(QUADS - 1)
                act.wait_ge(turns_in, 1)
                nc.scalar.activation(ang[:, 3:5, :], ang[:, 1:3, :], ACT.Sin, scale=TWO_PI_BELOW).then_inc(sin_done, 1)
                root(QUADS - 1)
                for i in range(KC):
                    act.wait_ge(ready["T"], KC + i + 1)
                    nc.scalar.copy(cT[:, i * TPB:(i + 1) * TPB, :],
                                   banks[early_bank("T1", i)].bitcast(F16).rearrange("p (t k) -> p t k", t=TPB)
                                   ).then_inc(cT_done, 1)
                x1_T(QUADS - 1)
                q_hi(QUADS - 1)
                m_copy(0, banks[early_bank("X", 0)])
                for i in range(KC):
                    k_hi(1, i, banks[early_bank("K1", i)])

                def body(b, u, s1, s2):
                    for t in range(KT):
                        exp(b, t)
                        for kind, i in plans[u][t]:
                            if kind == "V" and s2:
                                v_copy(b + 1, i, 1 - u, ring[slots[u][kind, i]])
                            if kind == "X" and s2:
                                m_copy(b + 1, ring[slots[u][kind, i]])
                        if not s2:
                            if t in X2T_STEPS:
                                x2_T(X2T_STEPS.index(t))
                    if s1:
                        for i in range(3):
                            k_hi(b + 2, i, ring[slots[u]["K", i]])

                def root_f(k, lo, hi, count):
                    act.wait_ge(ln_var[k], count)
                    nc.scalar.activation(std_f[:, k, lo:hi], mv_f[:, k, lo:hi, 1], ACT.Sqrt,
                                         bias=eps[:, 0:1]).then_inc(ln_std[k], 1)

                def x2_T(q):
                    act.wait_ge(x2T_ps, q + 1)
                    nc.scalar.copy(x2T[:, q, :], X2T_BANK).then_inc(x2T_sb, 1)

                for b in range(2):
                    body(b, b % 2, True, True)
                with act.Fori(1, B // 2 - 1) as i:
                    for u in range(2):
                        body(i * 2 + u, u, True, True)
                body(B - 2, 0, False, True)
                root_f(0, 0, 4 * LAST, 1)
                body(B - 1, 1, False, False)

                def turn(k):
                    act.wait_ge(h_ps, k + 1)
                    nc.scalar.activation(turns[:, k % FBUF, :], banks[k % G], ACT.Identity,
                                         bias=u_bias[:, k % G:k % G + 1], scale=0.1 * INV2PI).then_inc(turns_ready, 1)

                for k in range(AHEAD):
                    turn(k)
                for k in range(UNITS):
                    act.wait_ge(frac_ready, k + 1)
                    wait_past(act, z_ready, k - FBUF + 1)
                    nc.scalar.activation(sine[:, k % FBUF, :], turns[:, k % FBUF, :], ACT.Sin,
                                         scale=TWO_PI_BELOW).then_inc(sine_ready, 1)
                    if k + AHEAD < UNITS:
                        turn(k + AHEAD)
                    if k == ROOT_UNIT:
                        root_f(0, 4 * LAST, 4 * QUADS, 2)
                    if k == ROOT_UNIT + 2:
                        x2_T(LAST)
                root_f(1, 0, 4 * LAST, LAST)
                root_f(1, 4 * LAST, 4 * QUADS, QUADS)

            @block.tensor
            def _(pe):
                pe.wait_ge(pack_first, 16)
                for i, name in enumerate(("wqT", "wkT")):
                    nc.tensor.matmul(banks[2 + i], w(name), w("proj"), start=True, stop=True).then_inc(fold_ps, 1)
                pe.wait_ge(consts, 3)
                nc.tensor.matmul(banks[4][:, 0:P], ones[0:1, :], m["b_out_row"], start=True, stop=True)
                nc.tensor.matmul(banks[4][:, P:2 * P], ones[0:1, :], m["b2_row"], start=True,
                                 stop=True).then_inc(row_ps, 1)
                pe.wait_ge(fold_sb, 2)
                pe.wait_ge(row_done, 2)

                def x_T(q):
                    pe.wait_ge(xq_ready, q + 1)
                    for p in range(4):
                        last = nc.tensor.transpose(banks[0][:, p * P:(p + 1) * P], xq[:, p * D:(p + 1) * D], ident)
                    last.then_inc(xT_ps, 1)

                def values(q):
                    pe.wait_ge(xT_sb, q + 1)
                    for p in range(4):
                        last = nc.tensor.matmul(banks[0][:, p * P:(p + 1) * P], xT[:, p * P:(p + 1) * P], w("wv"),
                                                start=True, stop=True)
                    last.then_inc(v_ps, 1)

                def features(q, u):
                    wait_past(pe, feat_act, q * 8 + u - 3)
                    if u < 4:
                        mm = nc.tensor.matmul(banks[2 + u], xT[:, u * P:(u + 1) * P], wkp[:, :], start=True, stop=True)
                    else:
                        mm = nc.tensor.matmul(banks[u - 2], wqp[:, (u - 4) * P:(u - 3) * P], xT[:, :], start=True,
                                              stop=True)
                    mm.then_inc(feat_ps, 1)

                def key_values(q, i):
                    if i == 0:
                        pe.wait_ge(v_sb, 2 * q + 2)
                        wait_past(pe, aT_done, q)
                    pe.wait_ge(feat_done, q * 8 + 2 * i + 2)
                    if i:
                        pe.wait_ge(kv_sb, q * 2 + 1)
                    for p in (2 * i, 2 * i + 1):
                        for g in range(G):
                            last = nc.tensor.matmul(banks[6 + p % 2][:, 2 * KVW * g:2 * KVW * (g + 1)],
                                                    kf[:, p, g * P:(g + 1) * P],
                                                    v_s[:, p * G + g, :, :].rearrange("p e c -> p (e c)"),
                                                    start=True, stop=True)
                    last.then_inc(kv_ps, 1)

                def attend(q):
                    pe.wait_ge(feat_done, q * 8 + 8)
                    pe.wait_ge(kv_sb, q * 2 + 2)
                    for p in range(4):
                        for e in range(2):
                            tok = slice(p * P + SLOT * e, p * P + SLOT * e + SLOT)
                            for bank, sums in ((banks[6], kvn), (banks[7], kvd)):
                                for g in range(G):
                                    last = nc.tensor.matmul(bank[32 * g:32 * g + 32, tok],
                                                            sums[:, p // 2, p % 2, 2 * g + e, :], qf[:, g, tok],
                                                            start=True, stop=True)
                    last.then_inc(at_ps, 1)

                def out_projection(q):
                    pe.wait_ge(aT_done, q + 1)
                    for p in range(4):
                        last = nc.tensor.matmul(banks[1][:, p * P:(p + 1) * P], aT[:, p * P:(p + 1) * P], w("w_out"),
                                                start=True, stop=True)
                    last.then_inc(yo_ps, 1)

                def x1_T(q):
                    pe.wait_ge(x1_done, q + 1)
                    for p in range(4):
                        last = nc.tensor.transpose(banks[1][:, p * P:(p + 1) * P], x1[:, p * D:(p + 1) * D], ident)
                    last.then_inc(x1T_ps, 1)

                def queries(q):
                    pe.wait_ge(x1T_sb, q + 1)
                    nc.tensor.matmul(banks[1], w("WqT"), x1T[:, :], start=True, stop=True).then_inc(q_ps, 1)

                def front(q, back, ahead):
                    values(q)
                    for u in range(5):
                        features(q, u)
                    key_values(q, 0)
                    if back:
                        out_projection(q - 1)
                    features(q, 5)
                    features(q, 6)
                    key_values(q, 1)
                    features(q, 7)
                    if ahead:
                        attend(q)
                        if back:
                            x1_T(q - 1)
                        x_T(q + 1)
                        if back:
                            queries(q - 1)

                x_T(0)
                front(0, False, True)
                with pe.Fori(1, QUADS - 1) as q:
                    front(q, True, True)
                front(QUADS - 1, True, False)

                def unit(kind, i, n, u, bank, before):
                    if before is not None:
                        held, j, k = before
                        pe.wait_ge(DONE[held], k * PER[held] + j + 1)
                    if kind == "T":
                        if i == 0:
                            pe.wait_ge(c_split, n + 1)
                        out = bank.bitcast(F16).rearrange("p (t k) -> p t k", t=TPB)
                        for j in range(TPB):
                            last = nc.tensor.transpose(out[:, j, :], c_hl[:, i * TPB + j, :], ident16[:, :])
                    elif kind == "K":
                        if i == 0:
                            pe.wait_ge(cT_done, n * 3 + 3)
                        for k, (wt, part) in enumerate(((WkH, 0), (WkH, KT), (WkL, 0))):
                            last = nc.tensor.matmul(bank[:, 0:CH], wt[:, :],
                                                    cT[:, part + 4 * i:part + 4 * i + 4, 0:KP],
                                                    start=(k == 0), stop=(k == 2))
                    elif kind == "V":
                        for j in range(4):
                            for k, (part, wt) in enumerate(((0, WvH), (KT, WvH), (0, WvL))):
                                last = nc.tensor.matmul(bank[:, j * P:(j + 1) * P], cT[:, part + 4 * i + j, :],
                                                        wt[:, :], start=(k == 0), stop=(k == 2))
                    elif kind == "M":
                        r, c = divmod(i, KC)
                        if i == 0:
                            pe.wait_ge(kh_done, n * KC + KC)
                            pe.wait_ge(qm_ready, n + 1)
                        last = nc.tensor.matmul(bank[:, 0:CH], q_max[u][:, r * P:(r + 1) * P],
                                                kh[:, c * CH:(c + 1) * CH], start=True, stop=True)
                    elif kind == "X":
                        pe.wait_ge(m_cast, n + 1)
                        last = nc.tensor.transpose(bank.bitcast(F16)[0:MB, 0:P], m16[:, :], ident16[:, :])
                    elif kind == "R":
                        pe.wait_ge(o_copied, n + 1)
                        nc.tensor.matmul(bank[:, 0:3 * N], w("selA"), o_sb[:, u, 0:3 * N], start=True, stop=True)
                        last = nc.tensor.matmul(bank[:, 3 * N:GC], w("selB"), o_sb[:, u, 3 * N:GC], start=True,
                                                stop=True)
                    else:
                        pe.wait_ge(o_ready, n * 2 + 2)
                        for s in range(4):
                            last = nc.tensor.matmul(bank[:, 0:D], o_n[:, s, :, :].rearrange("p e n -> p (e n)"),
                                                    wslots[:, s, :], start=(s == 0), stop=(s == 3))
                    last.then_inc(ready[kind], 1)

                def score(b, t, u):
                    if t == 0:
                        pe.wait_ge(k_stacked, (b + 1) * 16 * 12)
                        pe.wait_ge(qd_ready, b + 1)
                        pe.wait_ge(m_placed, (b + 1) * 16)
                    wait_past(pe, p_ready, b * KT + t - 1)
                    for g in range(G):
                        last = nc.tensor.matmul(scores[t % 2][:, g // 2, (g % 2) * GC:(g % 2 + 1) * GC],
                                                k_stack[u][0:ROWS, g, t * KP:t * KP + P],
                                                q_diag[u][0:ROWS, g * GC:(g + 1) * GC], start=True, stop=True)
                    last.then_inc(s_ready, 1)

                def pv(b, t, u):
                    if t == 0:
                        pe.wait_ge(v_done, b * 3 + 3)
                        wait_past(pe, o_copied, b)
                    pe.wait_ge(p_ready, b * KT + t + 1)
                    for j in range(G):
                        at = j * GC
                        nc.tensor.matmul(O[32 * j:32 * j + 32, 0:3 * N], v_ext[u][0:KP, t, j, 0:32],
                                         probs[0:KP, t % PBUF, at:at + 3 * N], start=(t == 0), stop=(t == KT - 1),
                                         skip_group_check=True)
                    for j in range(G):
                        at = j * GC
                        last = nc.tensor.matmul(O[32 * j:32 * j + 16, 3 * N:GC], v_ext[u][0:KP, t, j, 32:48],
                                                probs[0:KP, t % PBUF, at + 3 * N:at + GC], start=False,
                                                stop=(t == KT - 1), skip_group_check=True)
                    last.then_inc(pv_done, 1)

                def body(b, pair, u, s1, s2, before):
                    held = [("X", 0, b)] * RING
                    for c in range(KC):
                        if s2:
                            held[slots[1 - u]["K", c]] = ("K", c, b + 1)

                    def go(kind, i):
                        n = {"T": b + 2, "K": b + 2, "R": b - 1, "Y": pair - 1}.get(kind, b + 1)
                        if {"T": s1, "K": s1, "R": before, "Y": before}.get(kind, s2):
                            slot = slots[u][kind, i]
                            unit(kind, i, n, u if kind in "TK" else 1 - u, ring[slot], held[slot])
                            held[slot] = (kind, i, n)

                    lag = 1 if s2 else 3
                    for t in range(KT):
                        score(b, t, u)
                        if not s2 and t in X2T_STEPS:
                            x2_T(X2T_STEPS.index(t))
                        half = (len(plans[u][t]) + 1) // 2
                        for kind, i in plans[u][t][:half]:
                            go(kind, i)
                        if t >= lag:
                            pv(b, t - lag, u)
                        for kind, i in plans[u][t][half:]:
                            go(kind, i)
                    for c in range(KC):
                        go("K", c)
                        if c < lag:
                            pv(b, KT - lag + c, u)

                def x2_T(q):
                    pe.wait_ge(x2_done, q + 1)
                    wait_past(pe, x2T_sb, q)
                    for p in range(4):
                        last = nc.tensor.transpose(X2T_BANK[:, p * P:(p + 1) * P], x_all[:, q, p * D:(p + 1) * D],
                                                   ident)
                    last.then_inc(x2T_ps, 1)

                def hidden(k):
                    q, g = divmod(k, G)
                    if g == 0:
                        pe.wait_ge(x2T_sb, q + 1)
                    wait_past(pe, z_ready, k - G + 1)
                    nc.tensor.matmul(banks[g], W1[:, g * P:(g + 1) * P], x2T[:, q, :], start=True,
                                     stop=True).then_inc(h_ps, 1)

                def project(k):
                    q, g = divmod(k, G)
                    pe.wait_ge(hid_ready, k + 1)
                    if g == 0:
                        wait_past(pe, y_done, q - 1)
                    for p in range(4):
                        last = nc.tensor.matmul(F_BANKS[q % 2][:, p * P:(p + 1) * P],
                                                hid[q % 2][:, g, p * P:(p + 1) * P], W2[:, g, :],
                                                start=(g == 0 and p == 0), stop=(g == G - 1), skip_group_check=True)
                    if g == G - 1:
                        last.then_inc(f_ps, 1)

                def early(kind, n, units):
                    for i in units:
                        bank = early_bank(kind, i)
                        unit(kind[0], i, n, n, banks[bank], held[bank])
                        held[bank] = (kind[0], i, n)

                held = [None] * 8
                pe.wait_ge(init, INIT)
                pe.wait_ge(pack_rest, 16)
                pe.wait_ge(split_done, 2)
                pe.wait_ge(feat_act, QUADS * 8)
                early("T", 0, range(KC))
                nc.tensor.matmul(banks[0][0:1, 0:P], w("bv"), w("WoT"), start=True, stop=True).then_inc(row_ps, 1)
                x1_T(QUADS - 2)
                early("K", 0, [0])
                queries(QUADS - 2)
                early("K", 0, range(1, KC))
                early("V", 0, range(KC))
                early("M", 0, range(0, 4))
                attend(QUADS - 1)
                early("M", 0, range(4, 8))
                out_projection(QUADS - 1)
                for i in range(8, 16):
                    early("M", 0, [i])
                    if i in T1_AFTER:
                        early("T1", 1, [T1_AFTER.index(i)])
                x1_T(QUADS - 1)
                early("M", 0, range(16, 19))
                queries(QUADS - 1)
                early("M", 0, range(19, NM))
                early("X", 0, [0])
                early("K1", 1, range(KC))
                pe.wait_ge(ql_done, QUADS)
                pe.wait_ge(row_done, 3)
                pe.wait_ge(o_zeroed, 1)
                for b in range(2):
                    body(b, 0, b % 2, True, True, b > 0)
                with pe.Fori(1, B // 2 - 1) as i:
                    for u in range(2):
                        body(i * 2 + u, i, u, True, True, True)
                for b in range(B - 2, B):
                    body(b, b // 2, b % 2, b + 2 < B, b + 1 < B, True)

                pe.wait_ge(p_ready, B * KT)
                for k in range(UNITS + PROJECT_LAG):
                    if k == G:
                        unit("R", 0, B - 1, 1, ring[END_SLOT], None)
                        unit("Y", 0, B // 2 - 1, 0, ring[END_SLOT], None)
                    if k == ROOT_UNIT + 5:
                        x2_T(LAST)
                    if k < UNITS:
                        hidden(k)
                    if k >= PROJECT_LAG:
                        project(k - PROJECT_LAG)

            @block.vector
            def _(dve):
                dve.memset(v_s[:, :, :, :], 0.0).then_inc(v_zeros, 1)
                dve.wait_ge(v_zeros, 1)
                for e in range(2):
                    dve.memset(v_s[SLOT * e:SLOT * e + N, :, e, 32:33], 1.0).then_inc(v_ones, 1)
                dve.memset(k_stack[0][96:97, :, :], SHIFT).then_inc(init, 1)
                dve.wait_ge(row_ps, 1)
                dve.tensor_copy(b_all[:, :], banks[4][:, 0:P]).then_inc(row_done, 1)
                dve.tensor_copy(b2_all[:, :], banks[4][:, P:2 * P]).then_inc(row_done, 1)
                dve.memset(k_stack[1][96:97, :, :], SHIFT).then_inc(init, 1)
                dve.memset(c_hl[96:P, :, :], 0.0).then_inc(c_zeroed, 1)

                def feature(q, u):
                    dve.wait_ge(feat_act, q * 8 + u + 1)
                    if u == 0:
                        wait_past(dve, kv_ps, q * 2)
                    if u == 4:
                        wait_past(dve, at_ps, q)
                    dst = kf[:, u, :] if u < 4 else qf[:, u - 4, :]
                    dve.scalar_tensor_tensor(dst, e_buf[:, u % 4, :], 1.0, relu_buf[:, u % 4, :], ALU.min,
                                             ALU.add).then_inc(feat_done, 1)

                def residual(q):
                    dve.wait_ge(yo_ps, q + 1)
                    dve.wait_ge(xres_ready, q + 1)
                    dve.tensor_tensor(xr[:, :], banks[1], xres[:, :], ALU.add).then_inc(xr_done, 1)
                    dve.wait_ge(xr_done, q + 1)
                    ln_stats(dve, xr, stats, mv, (ln1_stats, ln1_var, dve_settled), q)

                def normalise(q):
                    wait_past(dve, x1_kept, q)
                    ln_apply(dve, xr, x1, mv, std, rstd, ln1_std, ln1_rstd, q).then_inc(x1_done, 1)

                def key_values(q, i):
                    dve.wait_ge(kv_ps, q * 2 + i + 1)
                    if i == 0:
                        wait_past(dve, at_ps, q)
                    src = psum[:, 6:8, 0:8 * KVW].rearrange("p b (a c) -> p b a c", a=8)
                    dve.tensor_tensor(kvn[:, i, :, :, :], src[:, :, :, 0:32], mask_kv, ALU.mult)
                    dve.tensor_tensor(kvd[:, i, :, :, :], src[:, :, :, 32:33].to_broadcast([P, 2, 8, 32]), mask_kv,
                                      ALU.mult).then_inc(kv_sb, 1)

                def q_lo(q):
                    dve.wait_ge(qh_done, q + 1)
                    dve.scalar_tensor_tensor(ql[:, bass.ds(q * QT, QT)], banks[1], w("bq"),
                                             qh[:, bass.ds(q * QT, QT)], ALU.add, ALU.subtract).then_inc(ql_done, 1)

                def attend(q):
                    dve.wait_ge(den_done, q + 1)
                    dve.reciprocal(rden[:, :], den[:, :]).then_inc(rden_done, 1)
                    dve.wait_ge(rden_done, q + 1)
                    dve.tensor_tensor(aT[:, :], banks[6], rden[:, :], ALU.mult).then_inc(aT_done, 1)

                def front(q, back, last=False):
                    for u in range(5):
                        feature(q, u)
                    key_values(q, 0)
                    if back:
                        residual(q - 1)
                    feature(q, 5)
                    feature(q, 6)
                    key_values(q, 1)
                    feature(q, 7)
                    if back and not last:
                        normalise(q - 1)
                    if not last:
                        attend(q)
                    if back and not last:
                        q_lo(q - 1)

                front(0, False)
                dve.wait_ge(pack_rest, 16)
                for name, hi in (("WkT", WkH), ("WvT", WvH)):
                    dve.tensor_copy(hi[:, :], w(name)).then_inc(split_hi, 1)
                dve.tensor_copy(ident16[:, :], ident).then_inc(init, 1)
                dve.wait_ge(split_hi, 2)
                for name, hi, lo in (("WkT", WkH, WkL), ("WvT", WvH, WvL)):
                    dve.tensor_tensor(lo[:, :], w(name), hi[:, :], ALU.subtract).then_inc(split_done, 1)
                for t in k_stack:
                    dve.memset(t[0:96, :, S:S + 4], 0.0).then_inc(init, 1)
                dve.memset(o_n[:, :, :, :], 0.0).then_inc(init, 1)

                steps = [0]

                def chain(ins):
                    ins.then_inc(c_step, 1)
                    steps[0] += 1
                    dve.wait_ge(c_step, steps[0])

                theta = w("theta")
                n, f0, f1, sn, cs = (ang[:, i, :] for i in range(5))
                chain(dve.tensor_scalar(n, theta, INV2PI, None, ALU.mult))
                chain(dve.tensor_scalar(n, n, ROUND, -ROUND, ALU.add, ALU.add))
                chain(dve.scalar_tensor_tensor(theta_r[:, :], n, -C1, theta, ALU.mult, ALU.add))
                chain(dve.scalar_tensor_tensor(theta_r[:, :], n, -C2, theta_r[:, :], ALU.mult, ALU.add))
                chain(dve.scalar_tensor_tensor(theta_r[:, :], n, -C3, theta_r[:, :], ALU.mult, ALU.add))
                chain(dve.tensor_scalar(f0, theta_r[:, :], INV2PI, None, ALU.mult))
                chain(dve.scalar_tensor_tensor(u_bias[:, :], w("b1"), 0.1 * INV2PI, f0, ALU.mult, ALU.add))
                chain(dve.tensor_scalar(f0, f0, 0.5, -0.5, ALU.min, ALU.max))
                chain(dve.tensor_scalar(f1, f0, 0.25, None, ALU.add))
                chain(dve.tensor_scalar(n, f1, ROUND, -ROUND, ALU.add, ALU.add))
                dve.tensor_tensor(f1, f1, n, ALU.subtract).then_inc(turns_in, 1)

                front(1, True)
                with dve.Fori(2, QUADS - 1) as q:
                    front(q, True)
                front(QUADS - 1, True, True)

                def t_copy(n, i, bank):
                    dve.wait_ge(ready["T"], n * 3 + i + 1)
                    if i == 0:
                        wait_past(dve, ready["V"], n * 3)
                        wait_past(dve, ready["K"], n * 3)
                    dve.tensor_copy(cT[:, i * TPB:(i + 1) * TPB, :],
                                    bank.bitcast(F16).rearrange("p (t k) -> p t k", t=TPB)).then_inc(cT_done, 1)

                def k_lo(n, i, bank):
                    dve.wait_ge(kh_done, n * 3 + i + 1)
                    if i == 0:
                        wait_past(dve, k_stacked, n * 192)
                    dve.scalar_tensor_tensor(kl[:, i * CH:(i + 1) * CH], bank[:, 0:CH], w("bk"),
                                             kh[:, i * CH:(i + 1) * CH], ALU.add, ALU.subtract).then_inc(kl_done, 1)

                def m_max(n, i, bank):
                    dve.wait_ge(ready["M"], n * NM + i + 1)
                    if i == 0:
                        wait_past(dve, m_fold, n)
                    dve.tensor_reduce(mx[:, i:i + 1], bank[:, 0:CH], AX.X, ALU.max).then_inc(mx_done, 1)

                def m_row(n):
                    dve.wait_ge(mx_done, (n + 1) * NM)
                    dve.tensor_reduce(mrow[:, :], mx[:, :].rearrange("p (r c) -> p r c", c=KC), AX.X,
                                      ALU.max).then_inc(m_fold, 1)
                    dve.wait_ge(m_fold, n + 1)
                    wait_past(dve, ready["X"], n)
                    dve.tensor_scalar(m16[:, 0:MB], mrow[:, :], -1.0 / SHIFT, None, ALU.mult).then_inc(m_cast, 1)

                def invert(b, u, bank):
                    dve.wait_ge(ready["R"], b + 1)
                    dve.reciprocal(r_sb[:, u, :], bank[:, 0:GC]).then_inc(r_inv, 1)

                def scale_o(b, u):
                    dve.wait_ge(r_inv, b + 1)
                    dve.tensor_tensor(o_n[:, :, u, 0:N], o_sb[:, u, :].rearrange("p (s n) -> p s n", s=4),
                                      r_sb[:, u, :].rearrange("p (s n) -> p s n", s=4), ALU.mult).then_inc(o_ready, 1)

                def add_y(pair, bank):
                    dve.wait_ge(ready["Y"], pair + 1)
                    xs = x_pairs[:, bass.ds(pair, 1), :].rearrange("p o d -> p (o d)")
                    dve.tensor_tensor(xs, bank[:, 0:D], xs, ALU.add).then_inc(y_added, 1)

                def o_copy(b, u):
                    dve.wait_ge(pv_done, b * KT + KT)
                    dve.tensor_copy(o_sb[:, u, :], O[:, 0:GC]).then_inc(o_copied, 1)

                for i in range(KC):
                    t_copy(0, i, banks[early_bank("T", i)])
                normalise(QUADS - 2)
                k_lo(0, 0, banks[early_bank("K", 0)])
                q_lo(QUADS - 2)
                for i in range(1, KC):
                    k_lo(0, i, banks[early_bank("K", i)])
                dve.wait_ge(row_ps, 2)
                dve.tensor_tensor(wslots[0:1, 0, :], banks[0][0:1, 0:P], m["bo_row"], ALU.add).then_inc(row_done, 1)
                for i in range(NM):
                    m_max(0, i, banks[early_bank("M", i)])
                    if i == 3:
                        attend(QUADS - 1)
                        dve.memset(O, 0.0).then_inc(o_zeroed, 1)
                    if i == 9:
                        residual(QUADS - 1)
                    if i == 12:
                        normalise(QUADS - 1)
                m_row(0)
                q_lo(QUADS - 1)
                for i in range(KC):
                    k_lo(1, i, banks[early_bank("K1", i)])
                dve.wait_ge(sin_done, 1)
                chain(dve.tensor_tensor(ang[:, 5, :], cs, w("wr"), ALU.mult))
                chain(dve.tensor_tensor(ang[:, 6, :], sn, w("wi"), ALU.mult))
                chain(dve.tensor_tensor(ang[:, 5, :], ang[:, 5, :], ang[:, 6, :], ALU.add))
                chain(dve.scalar_tensor_tensor(s_coef[:, :], ang[:, 5, :], 0.1, w("wi"), ALU.mult, ALU.mult))

                def stats_of(k, pairs):
                    for a in pairs:
                        last = dve.bn_stats(stats_f[:, a, :], x_pairs[:, a, :])
                    last.then_inc(ln_stats_done[k], 1)

                def variances(k, pairs, count):
                    dve.wait_ge(ln_stats_done[k], count)
                    for a in pairs:
                        last = dve.bn_aggr(mv_f[:, k, a, :], stats_f[:, a, :])
                    last.then_inc(ln_var[k], 1)

                def invert_std(k, pairs, count):
                    dve.wait_ge(ln_std[k], count)
                    dve.reciprocal(rstd_f[:, k, pairs[0]:pairs[-1] + 1], std_f[:, k, pairs[0]:pairs[-1] + 1]
                                   ).then_inc(ln_rstd[k], 1)
                    dve.wait_ge(ln_rstd[k], count)

                def normalised(k, q):
                    for a in range(4 * q, 4 * q + 4):
                        last = dve.tensor_scalar(x_pairs[:, a, :], x_pairs[:, a, :], mv_f[:, k, a, 0:1],
                                                 rstd_f[:, k, a:a + 1], ALU.subtract, ALU.mult)
                    return last

                early = range(4 * LAST)

                def body(b, pair, u, s1, s2, before):
                    for t in range(KT):
                        for kind, i in plans[u][t]:
                            if kind in "MTRY":
                                bank = ring[slots[u][kind, i]]
                            if kind == "M" and s2:
                                m_max(b + 1, i, bank)
                                if i == NM - 1:
                                    m_row(b + 1)
                                    if not s1:
                                        dve.wait_ge(y_added, 4 * LAST)
                                        stats_of(0, early)
                                        variances(0, early, 1)
                            if kind == "T" and s1:
                                t_copy(b + 2, i, bank)
                            if kind == "R" and before:
                                invert(b - 1, 1 - u, bank)
                                scale_o(b - 1, 1 - u)
                            if kind == "Y" and before:
                                add_y(pair - 1, bank)
                    for i in range(KC):
                        if s1:
                            k_lo(b + 2, i, ring[slots[u]["K", i]])
                        if i == 0:
                            o_copy(b, u)

                for b in range(2):
                    body(b, 0, b, True, True, b > 0)
                with dve.Fori(1, B // 2 - 1) as i:
                    for u in range(2):
                        body(i * 2 + u, i, u, True, True, True)
                body(B - 2, B // 2 - 1, 0, False, True, True)
                invert_std(0, early, 1)
                for q in range(LAST):
                    normalised(0, q).then_inc(x2_done, 1)
                body(B - 1, B // 2 - 1, 1, False, False, True)

                def rounded(k):
                    dve.wait_ge(turns_ready, k + 1)
                    wait_past(dve, frac_ready, k - FBUF + 1)
                    dve.tensor_scalar(whole[:, k % FBUF, :], turns[:, k % FBUF, :], ROUND, -ROUND, ALU.add,
                                      ALU.add).then_inc(whole_ready, 1)

                def modulated(k):
                    dve.wait_ge(sine_ready, k + 1)
                    dve.scalar_tensor_tensor(z[:, k % FBUF, :], sine[:, k % FBUF, :], s_coef[:, k % G:k % G + 1],
                                             banks[k % G], ALU.mult, ALU.add).then_inc(z_ready, 1)

                def relu(k):
                    dve.wait_ge(z_ready, k + 1)
                    if k % G == 0:
                        wait_past(dve, f_ps, k // G - 1)
                    dve.tensor_scalar(hid[k // G % 2][:, k % G, :], z[:, k % FBUF, :], w("b1")[:, k % G:k % G + 1], 0.0,
                                      ALU.add, ALU.max).then_inc(hid_ready, 1)

                def sum3(q):
                    dve.wait_ge(f_ps, q + 1)
                    dve.wait_ge(x2b_done, q + 1)
                    dve.tensor_tensor(x_all[:, q, :], F_BANKS[q % 2], x_all[:, q, :], ALU.add).then_inc(y_done, 1)
                    dve.wait_ge(y_done, q + 1)
                    pairs = range(4 * q, 4 * q + 4)
                    stats_of(1, pairs)
                    variances(1, pairs, q + 1)

                last_pair, last_quad = B // 2 - 1, range(4 * LAST, 4 * QUADS)
                for k in range(AHEAD):
                    rounded(k)
                invert(B - 1, 1, ring[END_SLOT])
                scale_o(B - 1, 1)
                for k in range(UNITS):
                    modulated(k)
                    if k + AHEAD < UNITS:
                        rounded(k + AHEAD)
                    relu(k)
                    if k == 0:
                        add_y(last_pair, ring[END_SLOT])
                    if k == 1:
                        dve.wait_ge(y_added, last_pair + 1)
                        stats_of(0, last_quad)
                        variances(0, last_quad, 2)
                    if k == ROOT_UNIT:
                        invert_std(0, last_quad, 2)
                        normalised(0, LAST).then_inc(x2_done, 1)
                    if k >= G + 2 and k % G == 2:
                        sum3(k // G - 1)
                invert_std(1, early, 1)
                normalised(1, 0).then_inc(out_ready, 1)
                sum3(LAST)
                normalised(1, 1).then_inc(out_ready, 1)
                invert_std(1, last_quad, 2)
                normalised(1, LAST).then_inc(out_ready, 1)
                normalised(1, 2).then_inc(out_ready, 1)


def pack_inputs(i):
    t = {name: np.zeros((P, width), np.float32) for name, (_, width) in PACK.items()}
    f = {k: np.asarray(v) for k, v in i.items()}
    part = np.arange(P)
    t["ident"][part, part] = 1
    wqkv = f["L0_attn_w_qkv"]
    t["wqT"][:], t["wkT"][:], t["wv"][:] = wqkv[:, 0:D].T, wqkv[:, D:2 * D].T, wqkv[:, 2 * D:]
    for h in range(H):
        t["proj"][h * HD:(h + 1) * HD, h * FEAT:(h + 1) * FEAT] = f["L0_attn_proj_matrix"][h]
    t["w_out"][:] = f["L0_attn_w_out"]
    for name in ("Wq", "Wk", "Wv", "Wo"):
        t[name + "T"][:] = f["L0_xattn_" + name].T
    for h in range(H):
        j, s = divmod(h, 4)
        at = 32 * j + (8 + 8 * s if s < 3 else 0)
        t["WoSlots"][at:at + HD, s * P:(s + 1) * P] = f["L0_xattn_Wo"].T[h * HD:(h + 1) * HD]
    t["selA"][32 * (part // 32), part] = 1
    t["selB"][32 * (part // 32) + 8, part] = 1
    for h in range(4):
        t["maskKV"][32 * h:32 * h + 32, 8 * h:8 * h + 8] = 1
    for h in range(4):
        t["maskQ"][part % 32 // HD == h, h] = 1
    for h in range(H):
        t["maskM"][part // HD == h, h] = 1
    t["W1"][:] = f["L0_ffn_W1"]
    t["W2"][:] = f["L0_ffn_W2"].reshape(4, P, D).transpose(1, 0, 2).reshape(P, 4 * D)
    for name, key in (("bq", "L0_xattn_bq"), ("bk", "L0_xattn_bk"), ("bv", "L0_xattn_bv")):
        t[name][:, 0] = f[key]
    for name, key in (("b1", "L0_ffn_b1"), ("theta", "L0_ffn_quantum_phases"),
                      ("wr", "L0_ffn_quantum_weights_real"), ("wi", "L0_ffn_quantum_weights_imag")):
        t[name][:] = f[key].reshape(4, P).T
    for n, key in enumerate(("L0_attn_b_out", "L0_xattn_bo", "L0_ffn_b2")):
        t["rows"][0, n * P:(n + 1) * P] = f[key]
    return np.ascontiguousarray(np.concatenate([t[name] for name in PACK], axis=1))


def kernel(**inputs):
    import concourse.bacc as bacc
    from concourse.bass_utils import run_bass_kernel_spmd

    nc = bacc.Bacc("TRN2", target_bir_lowering=False, num_devices=1)
    arrays = {"ctx_in": np.ascontiguousarray(inputs["ctx_1024"]), "x_in": np.ascontiguousarray(inputs["x"]),
              "pack_in": pack_inputs(inputs)}
    drams = [nc.dram_tensor(name, a.shape, F32, kind="ExternalInput").ap() for name, a in arrays.items()]
    out = nc.dram_tensor("out", (B, N, D), F32, kind="ExternalOutput").ap()
    build(nc, *drams, out)
    return run_bass_kernel_spmd(nc, [arrays], core_ids=[0]).results[0]["out"]
```
